# Optimizing a Trainium2 kernel written in Bass

```python
import numpy as np
import jax
import jax.numpy as jnp

def _softmax(x, axis=-1):
    return jax.nn.softmax(x, axis=axis)

def _gelu(x):
    return jax.nn.gelu(x, approximate=True)

def _silu(x):
    return jax.nn.silu(x)

def _sigmoid(x):
    return jax.nn.sigmoid(x)

def _layernorm(x, axis=-1, eps=1e-05):
    m = jnp.mean(x, axis=axis, keepdims=True)
    v = jnp.var(x, axis=axis, keepdims=True)
    return (x - m) / jnp.sqrt(v + eps)

def _scatter_add(tgt, idx, src, axis=0):
    return tgt.at[idx].add(src)

def _segment_sum(src, seg, n):
    return jax.ops.segment_sum(src, seg, n)
kernel_name = 'mk_adaln_d1_jaxref_r4_fd60ef'

def setup_inputs(seed: int=0):
    np.random.seed(seed)
    _w = jnp.asarray

    def _L0_attn_setup():
        import jax, jax.numpy as jnp
        import numpy as np
        H = 16
        D_H = 128
        D_HR = 64
        THETA = 10000.0

        def rope(x, pos, theta=THETA):
            d = x.shape[-1]
            inv_freq = theta ** (-jnp.arange(0, d, 2, dtype=jnp.float32) / d)
            ang = pos.astype(jnp.float32)[:, None] * inv_freq[None, :]
            cos, sin = (jnp.cos(ang), jnp.sin(ang))
            x1, x2 = (x[..., 0::2], x[..., 1::2])
            out = jnp.stack([x1 * cos - x2 * sin, x1 * sin + x2 * cos], axis=-1)
            return out.reshape(x.shape)
        key = jax.random.key(seed)
        ks = jax.random.split(key, 9)
        d_model, d_latent = (512, 128)

        def w(k, shape):
            fan_in = shape[-1]
            return jax.random.normal(k, shape, dtype=jnp.float32) / jnp.sqrt(fan_in)
        return {'x': jax.random.normal(ks[0], (1, 512, d_model), dtype=jnp.float32), 'W_DQ': w(ks[1], (d_latent, d_model)), 'W_UQ': w(ks[2], (H * D_H, d_latent)), 'W_QR': w(ks[3], (H * D_HR, d_latent)), 'W_DKV': w(ks[4], (d_latent, d_model)), 'W_UK': w(ks[5], (H * D_H, d_latent)), 'W_UV': w(ks[6], (H * D_H, d_latent)), 'W_KR': w(ks[7], (D_HR, d_model)), 'W_O': w(ks[8], (d_model, H * D_H))}
    _L0_attn_in = _L0_attn_setup()

    def _L0_ffn_setup():
        import jax, jax.numpy as jnp
        import numpy as np
        TOP_K = 2
        key = jax.random.key(seed)
        ks = jax.random.split(key, 7)
        B, S, H = (2, 512, 512)
        E, A, NS = (8, 64, 4096)
        x = jax.random.normal(ks[0], (B, S, H), jnp.float32)
        gate_w = jax.random.normal(ks[1], (E, H), jnp.float32) * 0.01
        W = jax.random.normal(ks[2], (H, H), jnp.float32) * 0.02
        atoms = jax.random.normal(ks[3], (A, NS), jnp.float32) * 0.02
        expert_atom_weights = jax.random.normal(ks[4], (E, A), jnp.float32) * 0.1
        importance = jax.random.normal(ks[5], (E, NS), jnp.float32) * 0.1
        mask_idx = jax.random.randint(ks[6], (NS,), 0, H * H, jnp.int32)
        return dict(x=x, gate_w=gate_w, W=W, atoms=atoms, expert_atom_weights=expert_atom_weights, importance=importance, mask_idx=mask_idx)
    _L0_ffn_in = _L0_ffn_setup()
    _L0_c = _w((lambda *s: np.random.randn(*s).astype(np.float32) * 0.05)(8, 512))
    _L0_wmod = _w((lambda *s: np.random.randn(*s).astype(np.float32) * 0.05)(512, 6 * 512) * 512 ** (-0.5))
    _d = {'L0_attn_x': _L0_attn_in['x'], 'L0_attn_W_DQ': _L0_attn_in['W_DQ'], 'L0_attn_W_UQ': _L0_attn_in['W_UQ'], 'L0_attn_W_QR': _L0_attn_in['W_QR'], 'L0_attn_W_DKV': _L0_attn_in['W_DKV'], 'L0_attn_W_UK': _L0_attn_in['W_UK'], 'L0_attn_W_UV': _L0_attn_in['W_UV'], 'L0_attn_W_KR': _L0_attn_in['W_KR'], 'L0_attn_W_O': _L0_attn_in['W_O'], 'L0_ffn_gate_w': _L0_ffn_in['gate_w'], 'L0_ffn_W': _L0_ffn_in['W'], 'L0_ffn_atoms': _L0_ffn_in['atoms'], 'L0_ffn_expert_atom_weights': _L0_ffn_in['expert_atom_weights'], 'L0_ffn_importance': _L0_ffn_in['importance'], 'L0_ffn_mask_idx': _L0_ffn_in['mask_idx'], 'L0_c': _L0_c, 'L0_wmod': _L0_wmod}
    _x0 = _d['L0_attn_x']
    _d['L0_attn_x'] = jax.random.normal(jax.random.fold_in(jax.random.key(seed), 1), (8, 512, 512), dtype=_x0.dtype)
    del _x0
    return _d

def reference(L0_attn_x, L0_attn_W_DQ, L0_attn_W_UQ, L0_attn_W_QR, L0_attn_W_DKV, L0_attn_W_UK, L0_attn_W_UV, L0_attn_W_KR, L0_attn_W_O, L0_ffn_gate_w, L0_ffn_W, L0_ffn_atoms, L0_ffn_expert_atom_weights, L0_ffn_importance, L0_ffn_mask_idx, L0_c, L0_wmod):

    def _L0_attn_ref(x, W_DQ, W_UQ, W_QR, W_DKV, W_UK, W_UV, W_KR, W_O):
        import jax, jax.numpy as jnp
        import numpy as np
        H = 16
        D_H = 128
        D_HR = 64
        THETA = 10000.0

        def rope(x, pos, theta=THETA):
            d = x.shape[-1]
            inv_freq = theta ** (-jnp.arange(0, d, 2, dtype=jnp.float32) / d)
            ang = pos.astype(jnp.float32)[:, None] * inv_freq[None, :]
            cos, sin = (jnp.cos(ang), jnp.sin(ang))
            x1, x2 = (x[..., 0::2], x[..., 1::2])
            out = jnp.stack([x1 * cos - x2 * sin, x1 * sin + x2 * cos], axis=-1)
            return out.reshape(x.shape)
        B, S, _ = x.shape
        pos = jnp.arange(S)
        c_Q = x @ W_DQ.T
        q_C = (c_Q @ W_UQ.T).reshape(B, S, H, D_H).transpose(0, 2, 1, 3)
        q_R = (c_Q @ W_QR.T).reshape(B, S, H, D_HR).transpose(0, 2, 1, 3)
        q_R = rope(q_R, pos)
        q = jnp.concatenate([q_C, q_R], axis=-1)
        c_KV = x @ W_DKV.T
        k_C = (c_KV @ W_UK.T).reshape(B, S, H, D_H).transpose(0, 2, 1, 3)
        k_R = rope(x @ W_KR.T, pos)[:, None]
        k_R = jnp.broadcast_to(k_R, (B, H, S, D_HR))
        k = jnp.concatenate([k_C, k_R], axis=-1)
        v = (c_KV @ W_UV.T).reshape(B, S, H, D_H).transpose(0, 2, 1, 3)
        d_qk = D_H + D_HR
        scores = jnp.einsum('bhqd,bhkd->bhqk', q, k)
        scores = jnp.clip(scores, -80.0, 80.0)
        causal = pos[:, None] >= pos[None, :]
        scores = jnp.where(causal[None, None], scores, -jnp.inf)
        weights = jax.nn.softmax(scores / jnp.sqrt(jnp.float32(d_qk)), axis=-1)
        attn = jnp.einsum('bhqk,bhkd->bhqd', weights, v)
        out = attn.transpose(0, 2, 1, 3).reshape(B, S, H * D_H) @ W_O.T
        return out

    def _L0_ffn_ref(x, gate_w, W, atoms, expert_atom_weights, importance, mask_idx):
        import jax, jax.numpy as jnp
        import numpy as np
        TOP_K = 2
        B, S, H = x.shape
        xt = x.reshape(-1, H)
        logits = jnp.clip(xt @ gate_w.T, -50.0, 50.0)
        top_w, top_idx = jax.lax.top_k(logits, TOP_K)
        rw = jax.nn.softmax(top_w, axis=-1)
        deltas = jax.nn.softmax(expert_atom_weights, axis=-1) @ atoms
        weighted = deltas * jax.nn.sigmoid(importance)
        rows = mask_idx // H
        cols = mask_idx % H
        vals = jnp.einsum('tk,tks->ts', rw, weighted[top_idx])
        xg = xt[:, cols]
        contrib = jax.ops.segment_sum((xg * vals).T, rows, num_segments=H)
        out = xt @ W.T + contrib.T
        return out.reshape(B, S, H)
    x = L0_attn_x
    mod = (_silu(L0_c) @ L0_wmod).reshape(L0_c.shape[0], 6, 1, -1)
    sa, ca, ga, sb, cb, gb = (mod[:, 0], mod[:, 1], mod[:, 2], mod[:, 3], mod[:, 4], mod[:, 5])
    ga = (2 * (ga >= 0) - 1) * jnp.maximum(jnp.abs(ga), 0.25)
    gb = (2 * (gb >= 0) - 1) * jnp.maximum(jnp.abs(gb), 0.25)
    h = _layernorm(x, axis=-1) * (1 + ca) + sa
    x = x + ga * _L0_attn_ref(h, L0_attn_W_DQ, L0_attn_W_UQ, L0_attn_W_QR, L0_attn_W_DKV, L0_attn_W_UK, L0_attn_W_UV, L0_attn_W_KR, L0_attn_W_O)
    h = _layernorm(x, axis=-1) * (1 + cb) + sb
    x = x + gb * _L0_ffn_ref(h, L0_ffn_gate_w, L0_ffn_W, L0_ffn_atoms, L0_ffn_expert_atom_weights, L0_ffn_importance, L0_ffn_mask_idx)
    return x

_drawn_inputs = setup_inputs


def setup_inputs(seed=0):
    import zlib

    import numpy as np

    out = dict(_drawn_inputs(seed))
    spreads = {}
    factors = {'L0_ffn_gate_w': 64.0,
     'L0_ffn_atoms': 47.326,
     'L0_ffn_expert_atom_weights': 64.0,
     'L0_ffn_importance': 64.0}
    for name, (base, spread) in spreads.items():
        noise = np.random.default_rng([zlib.crc32(name.encode()), seed]).standard_normal(out[name].shape)
        drawn = base * np.exp(spread * noise) if base else spread * noise
        out[name] = jnp.asarray(drawn.astype(out[name].dtype))
    for name, factor in factors.items():
        out[name] = (out[name] * factor).astype(out[name].dtype)
    return out
```

```python
from contextlib import ExitStack

import concourse.bass as bass
from concourse import mybir

F32 = mybir.dt.float32
F32R = mybir.dt.float32r
I32 = mybir.dt.int32
U32 = mybir.dt.uint32
ALU = mybir.AluOpType
ACT = mybir.ActivationFunctionType
AX = mybir.AxisListType

B, S, D = 8, 512, 512
H, DH, DR, L = 16, 128, 64, 128
P = 128
NT = S // P
KT = D // P
E, NS, NA = 8, 4096, 64
ST = NS // P
NPAIR = H // 2
SCALE = float(DH + DR) ** -0.5
CLIP = 80.0
EPS = 1e-5
COL_BITS = D.bit_length() - 1
SCAT_B = ST // B

GROUPS = [[(0, 0)], [(1, 0), (3, S - P)], [(2, 0)]]
GCOLS = [S, S, S - 2 * P]
GOFF = [0, S, 2 * S]
PCOLS = sum(GCOLS)
PE_ORDER = [(0, 0, 0), (1, 1, 0), (1, 3, S - P), (2, 2, 0)]


STEPS = 4
NEWTON = 3 + 3 * STEPS


def linker(eng, semaphore, base, apart=None):
    count = [0]

    def link(ins):
        count[0] += 1
        ins.then_inc(semaphore, 1)
        eng.wait_ge(semaphore, base + (count[0] + 1))
        if apart:
            apart(eng)

    return link


def build(nc, x, wd, wuq, wuk, wuv, wqr, wo, gate, w, atoms, eaw, imp, idx_col, idx_row, c, wmod, consts, out):
    ctx = ExitStack()
    with ctx:
        def sb(name, shape, dt=F32):
            return ctx.enter_context(nc.sbuf_tensor(name, shape, dt))

        def sem(name):
            return ctx.enter_context(nc.semaphore(name))

        head_w = nc.dram_tensor("head_w", [H, P, 4, P], F32, kind="Internal").ap()
        gates_d = nc.dram_tensor("gates_d", [B, 2 * D], F32, kind="Internal").ap()
        x1_d = nc.dram_tensor("x1_d", [B * S, D], F32, kind="Internal").ap()
        table_d = nc.dram_tensor("table_d", [D * D + P, E], F32, kind="Internal").ap()

        arena = sb("arena", [P, 2 * KT * E * D], F32R)
        ew = arena[:, :].rearrange("p (s k e n) -> p s k e n", s=2, k=KT, e=E)
        cut = [0]

        def take(n):
            cut[0] += n
            assert cut[0] <= 2 * KT * E * D
            return arena[:, cut[0] - n:cut[0]]

        ow = take(2 * H * D).rearrange("p (s h n) -> p s h n", s=2, h=H)
        prob = take(4 * PCOLS).rearrange("p (b s n) -> p b s n", b=2, s=2)
        qs = take(8 * S).rearrange("p (b s n) -> p b s n", b=2, s=4)
        cq = take(2 * S).rearrange("p (s n) -> p s n", s=2)
        ckT = take(2 * S).rearrange("p (s n) -> p s n", s=2)
        ck = take(2 * S).rearrange("p (s t n) -> p s t n", s=2, t=NT)
        kr = take(2 * S).rearrange("p (s n) -> p s n", s=2)
        attn = take(4 * S).rearrange("p (j s n) -> p j s n", j=2, s=2)
        onesr = take(P)
        wstage = take(4 * P).rearrange("p (s n) -> p s n", s=4)
        h1r = arena[:, 2 * H * D:2 * H * D + 2 * KT * S].rearrange("p (s k n) -> p s k n", s=2, k=KT)
        hw = sb("hw", [P, 2, 4, P], F32R)
        wdr = sb("wdr", [P, 2, KT, 4, P], F32R)
        hTr = wdr[:, :, :, :, :].rearrange("p s k g n -> p (s k g n)")[:, 0:4 * KT * P].rearrange(
            "p (u s k n) -> p u s k n", u=2, s=2, k=KT)

        con = sb("con", [P, 5, S])
        cosin, coscos, sinsin, bound = con[:, 0, :], con[:, 1, :], con[:, 2, :], con[:, 3, :]
        ident, ones, later = con[:, 4, 0:P], con[:, 4, P:2 * P], con[:, 4, 2 * P:3 * P]
        iota8, trash = con[:, 4, 3 * P:3 * P + 8], con[:, 4, 3 * P + 8:3 * P + 9]
        work = sb("work", [P, 3 * NT * D])
        xb, xn, acc = (work[:, n * NT * D:(n + 1) * NT * D].rearrange("p (t n) -> p t n", t=NT) for n in range(3))
        rows = work[:, NT * D:3 * NT * D].bitcast(I32)
        rawf = work[:, NT * D:2 * NT * D].rearrange("p (u n) -> p u n", u=2)
        mrow, mrow2 = work[0:B, 2 * NT * D:2 * NT * D + 2 * D], work[0:B, 2 * NT * D + 2 * D:3 * NT * D]
        big = sb("big", [P, KT * S])
        h1 = big[:, :].rearrange("p (k n) -> p k n", k=KT)
        wdraw = big[:, :].rearrange("p (k g n) -> p k g n", k=KT, g=4)
        expo, qrot = big[:, 0:PCOLS], big[:, PCOLS:PCOLS + S]
        hT = big[:, 0:2 * KT * P].rearrange("p (u k n) -> p u k n", u=2, k=KT)
        clipped = sb("clipped", [P, PCOLS])
        ckv32, krot1, krot2 = clipped[:, 0:S], clipped[:, S:2 * S], big[:, PCOLS:PCOLS + S]
        recip = sb("recip", [P, S])
        attn32 = sb("attn32", [P, S])
        grow = sb("grow", [P, D])
        st6 = sb("st6", [P, NT, 6])
        mv = sb("mv", [P, NT, 2])
        rstd = sb("rstd", [P, NT])
        nr = sb("nr", [P, 3, NT])
        modT = sb("modT", [P, 4, KT, B])
        modb = sb("modb", [P, 4, KT])
        gate_sb = sb("gate_sb", [P, KT, E])
        cT = sb("cT", [P, 4, KT, B])
        atoms_sb = wdr_f = None
        went = sb("went", [P, ST, E])
        went2 = sb("went2", [P, ST, E])
        wcur = sb("wcur", [P, SCAT_B, E])
        smx = sb("smx", [E, 3, NA])
        sms = sb("sms", [E, 4])
        smT = sb("smT", [NA, E])
        sidx = sb("sidx", [P, 4, ST], I32)
        sidf = sb("sidf", [P, 5, ST])
        dest = sb("dest", [P, ST], U32)
        dcur = sb("dcur", [P, SCAT_B], U32)
        eq = attn32[:, :].rearrange("p (u a n) -> p u a n", u=2, a=2)
        top = sb("top", [P, 2, 8])
        topi = sb("topi", [P, 2, 8], U32)
        topf = sb("topf", [P, 2, 8])
        gw = sb("gw", [P, 2, 5])
        gt = sb("gt", [P, 2, 3, E])
        lg = sb("lg", [P, 2, E])
        atoms_sb = work[0:NA, 0:NS // 2]
        sig = clipped[:, 0:3 * ST * E].rearrange("p (a t e) -> p a t e", a=3, e=E)

        ps = ctx.enter_context(nc.psum_tensor("ps", [P, 8, S], F32))
        SC = [ps[:, 0, :], ps[:, 1, :], ps[:, 2, :]]
        QP, RP, VP, LP, OP = ps[:, 3, :], ps[:, 4, :], ps[:, 5, :], ps[:, 6, :], ps[:, 7, :]

        names = """con_in c_in wd_in wd_hi wd_lo g_in silu_e silu mod_in modT_mm modT_ev row_mm row_ev gates_out
            raw_in setA setB set_hi set_lo set_out
            eaw_in at_in at_mm imp_in imp_e sm_e sm sm_tr smT_ev ent idx_in rows_in eq eq_mm dest zero_set zero_out scat cur later x1g
            x_in ga_in modb norm tr h1_ev h1_hi h1_lo cq_mm ck_mm kr_mm cq_hi cq_lo ck_hi ck32 ck_lo ckt_mm ckt_hi ckt_lo kr_t kr_hi kr_lo
            q_mm qr_mm q_hi q_lo qr_t qr_hi qr_lo s_mm s_clip e32 e_hi e_lo pv_mm l_mm rec v_norm a_hi a_lo o_mm o_add acc0 x1 x1_out
            ch0 ch1 ch2 tab_in w_in ew_f ew_hi ew_lo gb_in modb2 xt_in xnorm2 tr2 h_ev h_hi h_lo lg_mm lg_d lg_e gates
            passed e_mm e_acc y y_out ones_r""".split()
        s = {n: sem(n) for n in names}
        counters = [n for n in names if not n.endswith(("_in", "_out")) and n not in ("scat", "passed")]

        def need(eng, name, n):
            eng.wait_ge(s[name], n + 1)

        def apart(eng):
            eng.sem_inc(s["passed"], 1)

        w_slot = [sem("head_w_in0"), sem("head_w_in1")]
        block = ctx.enter_context(nc.Block())

        x_t = x.rearrange("(b t p) d -> b p t d", t=NT, p=P)
        x1_t = x1_d.rearrange("(b t p) d -> b p t d", t=NT, p=P)
        x1_tile = x1_d.rearrange("(n p) d -> n p d", p=P)
        out_tile = out.rearrange("(n p) d -> n p d", p=P)
        wmod_t = wmod.rearrange("(k p) (g n) -> g p k n", p=P, g=6)
        wuq_t, wuk_t, wuv_t = (a.rearrange("(h d) l -> h d l", d=DH) for a in (wuq, wuk, wuv))
        wo_t = wo.rearrange("(h d) n -> h d n", d=DH)
        table_k = table_d[0:D * D, :].rearrange("(k p r) e -> k p (r e)", k=KT, p=P)

        xt = [xb[:, u, :] for u in range(2)]
        xnt = [xb[:, 2 + u, :] for u in range(2)]
        yt = [xn[:, u, :] for u in range(2)]
        accE = [xn[:, 2 + u, :] for u in range(2)]
        tab = work[:, NT * D:3 * NT * D]
        wrow = clipped[:, 0:D]
        ewf = big[:, :].rearrange("p (u n) -> p u n", u=4)[:, 0:2, :]

        @block.sync
        def _(sp):
            sp.dma_start(con[:, :, :], consts).then_inc(s["con_in"], 16)
            for name in counters:
                sp.sem_inc(s[name], 1)
            sp.dma_start(smx[:, 0, :], eaw).then_inc(s["eaw_in"], 16)
            sp.dma_start(sidx[:, 0, :], idx_col).then_inc(s["idx_in"], 16)
            sp.dma_start(rows, idx_row.partition_broadcast(P)).then_inc(s["rows_in"], 16)
            sp.dma_start(sig[:, 0, :, :].rearrange("p t e -> p (t e)"), imp).then_inc(s["imp_in"], 16)
            sp.dma_start(atoms_sb, atoms[:, 0:NS // 2]).then_inc(s["at_in"], 16)
            sp.dma_start(cT[:, 0, :, :], c.rearrange("(k p) b -> p k b", p=P)).then_inc(s["c_in"], 16)
            sp.dma_start(wdraw, wd.rearrange("(k p) g n -> p k g n", p=P)).then_inc(s["wd_in"], 16)
            sp.dma_start(gate_sb[:, :, :], gate.rearrange("(k p) e -> p k e", p=P)).then_inc(s["g_in"], 16)
            need(sp, "zero_set", 1)
            for k in range(KT):
                sp.dma_start(table_k[k].rearrange("p (r n) -> p r n", n=S),
                             recip.rearrange("p (r n) -> p r n", r=1).broadcast_to([P, E, S])).then_inc(s["zero_out"], 16)
            sp.dma_start(table_d[D * D:D * D + P, :], recip[:, 0:E]).then_inc(s["zero_out"], 16)
            need(sp, "at_mm", 1)
            sp.dma_start(atoms_sb, atoms[:, NS // 2:NS]).then_inc(s["at_in"], 16)
            need(sp, "at_mm", 2)
            for g in range(6):
                if g:
                    need(sp, "modT_mm", g)
                sp.dma_start(xb, wmod_t[g]).then_inc(s["mod_in"], 16)
            need(sp, "row_ev", 2)
            sp.dma_start(gates_d, mrow).then_inc(s["gates_out"], 16)
            need(sp, "dest", 1)

            def head_raw(h, u, stored):
                for n, src in enumerate((wuq_t, wuk_t, wuv_t)):
                    sp.dma_start(rawf[:, u, n * L:(n + 1) * L], src[h]).then_inc(s["raw_in"], 16)
                sp.dma_start(rawf[:, u, 3 * L:3 * L + D], wo_t[h]).then_inc(s["raw_in"], 16)
                sp.dma_start(rawf[:, u, 3 * L + D:4 * L + D], wqr[h]).then_inc(s["raw_in"], 16)

            with sp.Fori(0, H) as h:
                need(sp, "set_hi", h * 3)
                need(sp, "set_lo", h * 3)
                head_raw(h, 0, None)
                need(sp, "set_hi", h * 3 + 3)
                need(sp, "set_lo", h * 3 + 3)
                sp.dma_start(head_w[h], wstage.bitcast(F32)).then_inc(s["set_out"], 16)
                sp.wait_ge(s["set_out"], h * 16 + 16)
                apart(sp)
            sp.wait_ge(s["gates_out"], 16)

            for slot in range(2):
                sp.dma_start(hw[:, slot].bitcast(F32), head_w[slot]).then_inc(w_slot[slot], 16)

            def next_weights(used, head, slot):
                need(sp, "qr_mm", used)
                sp.dma_start(hw[:, slot].bitcast(F32), head_w[head]).then_inc(w_slot[slot], 16)

            with sp.Fori(0, B) as b:
                need(sp, "x1", b)
                sp.dma_start(xb, x_t[b]).then_inc(s["x_in"], 16)
                sp.dma_start(grow[:, :], gates_d[b, 0:D].partition_broadcast(P)).then_inc(s["ga_in"], 16)
                with sp.Fori(0, NPAIR - 1) as p:
                    for j in range(2):
                        next_weights(b * H + p * 2 + (j + 1), p * 2 + (j + 2), j)
                for j in range(2):
                    next_weights(b * H + (H - 1 + j), j, j)
                need(sp, "x1", b + 1)
                sp.dma_start(x1_t[b], acc).then_inc(s["x1_out"], 16)
            sp.wait_ge(s["x1_out"], B * 16)
            for slot in range(2):
                sp.wait_ge(w_slot[slot], 16 * (B * NPAIR + 1))

            sp.wait_ge(s["scat"], 16 * ST)
            need(sp, "acc0", B + 1)
            with sp.Fori(0, KT) as k:
                need(sp, "ew_lo", k * E)
                sp.dma_start(tab, table_k[k]).then_inc(s["tab_in"], 16)
                sp.dma_start(wrow, w.rearrange("(k p) n -> k p n", p=P)[k]).then_inc(s["w_in"], 16)
            need(sp, "ew_lo", KT * E)
            with sp.Fori(0, B) as b:
                need(sp, "y", b * NT)
                sp.dma_start(grow[:, :], gates_d[b, D:2 * D].partition_broadcast(P)).then_inc(s["gb_in"], 16)
                with sp.Fori(0, NT // 2) as m:
                    need(sp, "y", b * NT + m * 2)
                    for u in range(2):
                        sp.dma_start(xt[u], x1_tile[b * NT + m * 2 + u]).then_inc(s["xt_in"], 16)
                    for u in range(2):
                        need(sp, "y", b * NT + m * 2 + (u + 1))
                        sp.dma_start(out_tile[b * NT + m * 2 + u], yt[u]).then_inc(s["y_out"], 16)
                    sp.wait_ge(s["y_out"], (b * NT + m * 2 + 2) * 16)
                    apart(sp)
            sp.wait_ge(s["y_out"], 16 * B * NT)

        @block.gpsimd
        def _(pool):
            pool.memset(recip[:, :], 0.0).then_inc(s["zero_set"], 1)
            pool.wait_ge(s["zero_out"], 16 * (KT + 1))
            need(pool, "dest", 1)
            pool.wait_ge(s["gates_out"], 16)

            def low_rope(head, parity):
                need(pool, "qr_hi", head + 1)
                pool.tensor_tensor(qs[:, parity, 3, :], qrot, qs[:, parity, 2, :].bitcast(F32), ALU.subtract).then_inc(s["qr_lo"], 1)

            def low_attn(head, j):
                need(pool, "a_hi", head + 1)
                pool.tensor_tensor(attn[:, j, 1, :], attn32[:, :], attn[:, j, 0, :].bitcast(F32), ALU.subtract).then_inc(s["a_lo"], 1)

            pool.memset(acc, 0.0).then_inc(s["acc0"], 1)
            with pool.Fori(0, B) as b:
                pool.tensor_copy(dcur[:, :], dest[:, bass.ds(b * SCAT_B, SCAT_B)]).then_inc(s["cur"], 1)
                pool.tensor_copy(wcur[:, :, :], went2[:, bass.ds(b * SCAT_B, SCAT_B), :]).then_inc(s["cur"], 1)
                need(pool, "cur", b * 2 + 2)
                apart(pool)
                for n in range(SCAT_B):
                    pool.indirect_dma_start(table_d, bass.IndirectOffsetOnAxis(ap=dcur[:, n:n + 1], axis=0), wcur[:, n, :], None,
                                            compute_op=ALU.add).then_inc(s["scat"], 16)
                    pool.wait_ge(s["scat"], (b * SCAT_B + (n + 1)) * 16)
                    apart(pool)
                low_rope(b * H, 0)
                low_rope(b * H + 1, 1)
                with pool.Fori(1, NPAIR) as p:
                    h = b * H + p * 2
                    low_rope(h, 0)
                    low_attn(h - 2, 0)
                    low_rope(h + 1, 1)
                    low_attn(h - 1, 1)
                low_attn(b * H + (H - 2), 0)
                low_attn(b * H + (H - 1), 1)
                pool.wait_ge(s["x1_out"], b * 16 + 16)
                apart(pool)
                pool.memset(acc, 0.0).then_inc(s["acc0"], 1)

        @block.scalar
        def _(act):
            def copy(dst, src, done):
                act.activation(dst, src, ACT.Copy).then_inc(s[done], 1)

            need(act, "sm", 1)
            act.activation(smx[:, 1, :], smx[:, 0, :], ACT.Exp, bias=sms[:, 0:1], accum_out=sms[:, 1:2]).then_inc(s["sm_e"], 1)
            act.wait_ge(s["imp_in"], 16)
            act.activation(sig[:, 1, :, :], sig[:, 0, :, :], ACT.Exp, scale=-1.0).then_inc(s["imp_e"], 1)
            act.wait_ge(s["c_in"], 16)
            act.activation(cT[:, 1, :, :], cT[:, 0, :, :], ACT.Exp, scale=-1.0).then_inc(s["silu_e"], 1)
            act.wait_ge(s["wd_in"], 16)
            copy(wdr[:, 0], wdraw, "wd_hi")
            with act.Fori(0, H) as h:
                act.wait_ge(s["raw_in"], h * 80 + 80)
                copy(wstage[:, 2, :], rawf[:, 0, 3 * L + D:4 * L + D], "set_hi")
                need(act, "setA", h + 1)
                copy(wstage[:, 0, :], QP[:, 0:P], "set_hi")
                need(act, "setB", h + 1)
                act.activation(ow[:, 0, h, :], RP, ACT.Copy).then_inc(s["set_hi"], 1)

            def high_query(head, parity):
                need(act, "q_mm", head + 1)
                copy(qs[:, parity, 0, :], QP, "q_hi")
                need(act, "qr_t", head + 1)
                copy(qs[:, parity, 2, :], qrot, "qr_hi")

            def exps(head, parity):
                for g in range(3):
                    cols = slice(GOFF[g], GOFF[g] + GCOLS[g])
                    need(act, "s_clip", head * 3 + (g + 1))
                    act.activation(expo[:, cols], clipped[:, cols], ACT.Exp, scale=SCALE).then_inc(s["e32"], 1)
                    act.activation(prob[:, parity, 0, cols], clipped[:, cols], ACT.Exp, scale=SCALE).then_inc(s["e_hi"], 1)

            def high_attn(head, j):
                need(act, "v_norm", head + 1)
                copy(attn[:, j, 0, :], attn32[:, :], "a_hi")

            with act.Fori(0, B) as b:
                for k in range(KT):
                    need(act, "tr", b * KT + (k + 1))
                    if k == 0:
                        need(act, "modb", b + 1)
                        need(act, "h1_lo", b * KT)
                    act.activation(h1[:, k, :], [SC[0], SC[1], SC[2], OP][k], ACT.Identity,
                                   bias=modb[:, 0, k:k + 1], scale=modb[:, 1, k:k + 1]).then_inc(s["h1_ev"], 1)
                    need(act, "h1_ev", b * KT + (k + 1))
                    copy(h1r[:, 0, k, :], h1[:, k, :], "h1_hi")
                need(act, "cq_mm", b + 1)
                copy(cq[:, 0, :], QP, "cq_hi")
                need(act, "ck_mm", b + 1)
                copy(ckT[:, 0, :], RP, "ck_hi")
                need(act, "ck_hi", b + 1)
                copy(ckv32, RP, "ck32")
                need(act, "ckt_mm", b + 1)
                act.activation(ck[:, 0, :, :], LP.rearrange("p (t n) -> p t n", t=NT), ACT.Copy).then_inc(s["ckt_hi"], 1)
                need(act, "kr_t", b + 1)
                copy(kr[:, 0, :], krot1, "kr_hi")
                h = b * H
                high_query(h, 0)
                high_query(h + 1, 1)
                exps(h, 0)
                high_query(h + 2, 0)
                exps(h + 1, 1)
                high_attn(h, 0)
                with act.Fori(1, NPAIR - 1) as p:
                    h = b * H + p * 2
                    high_query(h + 1, 1)
                    exps(h, 0)
                    high_attn(h - 1, 1)
                    high_query(h + 2, 0)
                    exps(h + 1, 1)
                    high_attn(h, 0)
                h = b * H + (H - 2)
                high_query(h + 1, 1)
                exps(h, 0)
                high_attn(h - 1, 1)
                exps(h + 1, 1)
                high_attn(h, 0)
                high_attn(h + 1, 1)

            with act.Fori(0, KT) as k:
                for e in range(E):
                    need(act, "ew_f", k * E + (e + 1))
                    act.activation(ew[:, 0, k, e, :], ewf[:, e % 2, :], ACT.Copy).then_inc(s["ew_hi"], 1)
            with act.Fori(0, B) as b:
                need(act, "modb2", b + 1)
                with act.Fori(0, NT // 2) as m:
                    for u in range(2):
                        t = b * NT + m * 2 + u
                        need(act, "tr2", t + 1)
                        for k in range(KT):
                            act.activation(hT[:, u, k, :], ps[:, 6, k * P:(k + 1) * P], ACT.Identity,
                                           bias=modb[:, 2, k:k + 1], scale=modb[:, 3, k:k + 1]).then_inc(s["h_ev"], 1)
                        need(act, "h_ev", t * KT + KT)
                        act.activation(hTr[:, u, 0, :, :], hT[:, u, :, :], ACT.Copy).then_inc(s["h_hi"], 1)
                        need(act, "lg_d", t + 1)
                        act.activation(gw[:, u, 1:2], gw[:, u, 0:1], ACT.Exp).then_inc(s["lg_e"], 1)

        @block.tensor
        def _(pe):
            def split3(o, wgt, act_, first=True, last=True):
                pe.matmul(o, wgt(0), act_(0), start=first, stop=False)
                pe.matmul(o, wgt(1), act_(0), start=False, stop=False)
                return pe.matmul(o, wgt(0), act_(1), start=False, stop=last)

            pe.wait_ge(s["con_in"], 16)
            need(pe, "sm", 2)
            pe.transpose(VP[0:NA, 0:E], smx[:, 2, :], ident[0:E, 0:E]).then_inc(s["sm_tr"], 1)
            need(pe, "smT_ev", 1)
            for half in range(2):
                pe.wait_ge(s["at_in"], 16 * (half + 1))
                for n in range(ST // 2):
                    t = half * (ST // 2) + n
                    mm = pe.matmul(SC[0][:, t * E:(t + 1) * E], atoms_sb[:, n * P:(n + 1) * P], smT[:, :], start=True, stop=True)
                mm.then_inc(s["at_mm"], 1)
            need(pe, "ent", 1)
            with pe.Fori(0, ST // 2) as m:
                for u in range(2):
                    need(pe, "eq", m * 2 + (u + 1))
                    pe.matmul(SC[1 + u][:, bass.ds(m * E, E)], eq[:, u, 0, :], went[:, m * 2 + u, :], start=True, stop=True).then_inc(s["eq_mm"], 1)
            need(pe, "silu", 1)
            for g in range(6):
                pe.wait_ge(s["mod_in"], 16 * (g + 1))
                if g in (2, 5):
                    for k in range(KT):
                        mm = pe.matmul((QP, RP)[g // 3][0:B, :], cT[:, 3, k, :], xb[:, k, :], start=(k == 0), stop=(k == KT - 1))
                else:
                    n = g if g < 2 else g - 1
                    for m in range(KT):
                        for k in range(KT):
                            mm = pe.matmul(VP[:, (n * KT + m) * B:(n * KT + m + 1) * B], xb[:, k, m * P:(m + 1) * P], cT[:, 3, k, :],
                                           start=(k == 0), stop=(k == KT - 1))
                mm.then_inc(s["modT_mm"], 1)
            need(pe, "row_ev", 2)
            with pe.Fori(0, H) as h:
                pe.wait_ge(s["raw_in"], h * 80 + 80)
                need(pe, "set_hi", h * 3)
                need(pe, "set_lo", h * 3)
                pe.matmul(QP[:, 0:P], rawf[:, 0, 0:L], rawf[:, 0, L:2 * L], start=True, stop=True).then_inc(s["setA"], 1)
                pe.matmul(RP, rawf[:, 0, 2 * L:3 * L], rawf[:, 0, 3 * L:3 * L + D], start=True, stop=True).then_inc(s["setB"], 1)
            need(pe, "set_hi", 3 * H)
            need(pe, "set_lo", 3 * H)
            need(pe, "wd_lo", 1)
            need(pe, "ones_r", 1)

            def queries(head, parity, nw):
                pe.wait_ge(w_slot[parity], nw * 16 + 16)
                need(pe, "q_hi", head)
                need(pe, "q_lo", head)
                split3(QP, lambda i: hw[:, parity, i, :], lambda i: cq[:, i, :]).then_inc(s["q_mm"], 1)
                need(pe, "qr_t", head)
                split3(RP, lambda i: hw[:, parity, 2 + i, :], lambda i: cq[:, i, :]).then_inc(s["qr_mm"], 1)

            def scores(head, parity, g):
                if g == 0:
                    need(pe, "q_lo", head + 1)
                    need(pe, "qr_lo", head + 1)
                need(pe, "s_clip", head * 3)
                for i, c0 in GROUPS[g]:
                    n = S - i * P
                    o = SC[g][:, c0:c0 + n]
                    keys = slice(i * P, (i + 1) * P)
                    split3(o, lambda k: ckT[:, k, keys], lambda k: qs[:, parity, k, i * P:S], last=False)
                    mm = split3(o, lambda k: kr[:, k, keys], lambda k: qs[:, parity, 2 + k, i * P:S], first=False)
                mm.then_inc(s["s_mm"], 1)

            def values(head, parity):
                need(pe, "v_norm", head)
                for n, (g, i, c0) in enumerate(PE_ORDER):
                    if n != 2:
                        need(pe, "e_lo", head * 3 + (g + 1))
                    cols = slice(GOFF[g] + c0, GOFF[g] + c0 + S - i * P)
                    mm = split3(VP[:, i * P:S], lambda k: ck[:, k, i, :], lambda k: prob[:, parity, k, cols], first=(n == 0), last=(n == 3))
                mm.then_inc(s["pv_mm"], 1)
                for n, (g, i, c0) in enumerate(PE_ORDER):
                    cols = slice(GOFF[g] + c0, GOFF[g] + c0 + S - i * P)
                    for k in range(2):
                        mm = pe.matmul(LP[:, i * P:S], onesr, prob[:, parity, k, cols], start=(n == 0 and k == 0), stop=(n == 3 and k == 1))
                mm.then_inc(s["l_mm"], 1)

            def project(pair, p, t):
                if t == 0:
                    need(pe, "a_lo", pair * 2 + 2)
                need(pe, "o_add", pair * NT + t)
                for j in range(2):
                    mm = split3(OP, lambda k: attn[:, j, k, t * P:(t + 1) * P], lambda k: ow[:, k, p * 2 + j, :], first=(j == 0), last=(j == 1))
                mm.then_inc(s["o_mm"], 1)

            with pe.Fori(0, B) as b:
                need(pe, "norm", b * NT + NT)
                need(pe, "o_add", b * (NPAIR * NT))
                for k in range(KT):
                    bank = [SC[0], SC[1], SC[2], OP][k]
                    for t in range(NT):
                        mm = pe.transpose(bank[:, t * P:(t + 1) * P], xn[:, t, k * P:(k + 1) * P], ident)
                    mm.then_inc(s["tr"], 1)
                banks = [QP, RP, VP, LP]
                for g, done in enumerate(("cq_mm", "ck_mm", "kr_mm", "kr_mm")):
                    for k in range(KT):
                        if g == 0:
                            need(pe, "h1_lo", b * KT + (k + 1))
                        mm = split3(banks[g], lambda i: wdr[:, i, k, g, :], lambda i: h1r[:, i, k, :], first=(k == 0), last=(k == KT - 1))
                    mm.then_inc(s[done], 1)
                need(pe, "ck32", b + 1)
                need(pe, "kr_t", b + 1)
                for t in range(NT):
                    mm = pe.transpose(LP[:, t * P:(t + 1) * P], ckv32[:, t * P:(t + 1) * P], ident)
                mm.then_inc(s["ckt_mm"], 1)
                need(pe, "cq_lo", b + 1)
                need(pe, "ck_lo", b + 1)
                nw = b * NPAIR
                h = b * H
                queries(h, 0, nw)
                queries(h + 1, 1, nw)
                need(pe, "kr_lo", b + 1)
                for g in range(3):
                    scores(h, 0, g)
                queries(h + 2, 0, nw + 1)
                for g in range(3):
                    scores(h + 1, 1, g)
                need(pe, "ckt_lo", b + 1)
                values(h, 0)
                with pe.Fori(1, NPAIR - 1) as p:
                    h = b * H + p * 2
                    pair = b * NPAIR + p
                    queries(h + 1, 1, pair)
                    for g in range(3):
                        scores(h, 0, g)
                    values(h - 1, 1)
                    queries(h + 2, 0, pair + 1)
                    for g in range(3):
                        scores(h + 1, 1, g)
                        project(pair - 1, p - 1, g)
                    project(pair - 1, p - 1, 3)
                    values(h, 0)
                h = b * H + (H - 2)
                pair = b * NPAIR + (NPAIR - 1)
                queries(h + 1, 1, pair)
                for g in range(3):
                    scores(h, 0, g)
                values(h - 1, 1)
                for g in range(3):
                    scores(h + 1, 1, g)
                    project(pair - 1, NPAIR - 2, g)
                project(pair - 1, NPAIR - 2, 3)
                values(h, 0)
                values(h + 1, 1)
                for t in range(NT):
                    project(pair, NPAIR - 1, t)

            need(pe, "ew_lo", KT * E)
            need(pe, "ew_hi", KT * E)
            pe.wait_ge(s["g_in"], 16)
            with pe.Fori(0, B) as b:
                with pe.Fori(0, NT // 2) as m:
                    for u in range(2):
                        t = b * NT + m * 2 + u
                        need(pe, "xnorm2", t + 1)
                        need(pe, "h_ev", t * KT)
                        for k in range(KT):
                            mm = pe.transpose(ps[:, 6, k * P:(k + 1) * P], xnt[u][:, k * P:(k + 1) * P], ident)
                        mm.then_inc(s["tr2"], 1)
                        need(pe, "h_lo", t + 1)
                        need(pe, "gates", t)
                        for k in range(KT):
                            mm = pe.matmul(ps[:, 7, 0:E], hT[:, u, k, :], gate_sb[:, k, :], start=(k == 0), stop=(k == KT - 1))
                        mm.then_inc(s["lg_mm"], 1)
                        for e in range(E):
                            if e < 4:
                                need(pe, "e_acc", t * E)
                            else:
                                need(pe, "e_acc", t * E + (e - 3))
                            for k in range(KT):
                                mm = split3(ps[:, e % 4, :], lambda i: hTr[:, u, i, k, :], lambda i: ew[:, i, k, e, :],
                                            first=(k == 0), last=(k == KT - 1))
                            mm.then_inc(s["e_mm"], 1)

        @block.vector
        def _(dve):
            V = nc.vector
            link = linker(dve, s["ch0"], 0)
            dve.wait_ge(s["con_in"], 16)
            V.tensor_copy(onesr, ones).then_inc(s["ones_r"], 1)
            dve.wait_ge(s["eaw_in"], 16)
            link(V.tensor_reduce(sms[:, 2:3], smx[:, 0, :], AX.X, ALU.max))
            V.tensor_scalar(sms[:, 0:1], sms[:, 2:3], -1.0, None, ALU.mult).then_inc(s["sm"], 1)
            need(dve, "sm_e", 1)
            link(V.reciprocal(sms[:, 3:4], sms[:, 1:2]))
            V.tensor_scalar(smx[:, 2, :], smx[:, 1, :], sms[:, 3:4], None, ALU.mult).then_inc(s["sm"], 1)
            need(dve, "sm_tr", 1)
            V.tensor_copy(smT[:, :], VP[0:NA, 0:E]).then_inc(s["smT_ev"], 1)
            need(dve, "imp_e", 1)
            link(V.tensor_scalar(sig[:, 2, :, :], sig[:, 1, :, :], 1.0, None, ALU.add))
            link(V.reciprocal(sig[:, 1, :, :], sig[:, 2, :, :]))
            need(dve, "at_mm", 2)
            V.tensor_tensor(went[:, :, :].rearrange("p t e -> p (t e)"), SC[0][:, 0:ST * E], sig[:, 1, :, :].rearrange("p t e -> p (t e)"), ALU.mult).then_inc(s["ent"], 1)
            dve.wait_ge(s["idx_in"], 16)
            link(V.tensor_scalar(sidx[:, 1, :], sidx[:, 0, :], D - 1, COL_BITS, ALU.bitwise_and, ALU.logical_shift_left))
            link(V.tensor_scalar(sidx[:, 2, :], sidx[:, 0, :], COL_BITS, None, ALU.logical_shift_right))
            link(V.tensor_tensor(sidx[:, 3, :], sidx[:, 1, :], sidx[:, 2, :], ALU.bitwise_or))
            link(V.tensor_copy(sidf[:, 0, :], sidx[:, 3, :]))
            link(V.tensor_copy(sidf[:, 1, :], sidx[:, 0, :]))
            dve.wait_ge(s["rows_in"], 16)
            with dve.Fori(0, ST // 2) as m:
                need(dve, "eq_mm", m * 2)
                need(dve, "later", m * 2)
                for u in range(2):
                    here = rows[:, bass.ds((m * 2 + u) * P, P)]
                    col = sidf[:, 1, bass.ds(m * 2 + u, 1)]
                    V.tensor_scalar(eq[:, u, 0, :], here, col, None, ALU.is_equal).then_inc(s["eq"], 1)
                    V.scalar_tensor_tensor(out=eq[:, u, 1, :], in0=here, scalar=col, in1=later, op0=ALU.is_equal, op1=ALU.mult,
                                           accum_out=sidf[:, 2, bass.ds(m * 2 + u, 1)]).then_inc(s["later"], 1)
            need(dve, "later", ST)
            need(dve, "eq_mm", ST)
            w2 = went2[:, :, :].rearrange("p (m u) e -> p u m e", u=2)
            for u in range(2):
                link(V.tensor_copy(w2[:, u], SC[1 + u][:, 0:ST // 2 * E].rearrange("p (m e) -> p m e", e=E)))
            link(V.tensor_scalar(sidf[:, 3, :], sidf[:, 2, :], 0.0, None, ALU.is_gt))
            link(V.tensor_scalar(sidf[:, 2, :], sidf[:, 0, :], trash, None, ALU.subtract))
            link(V.tensor_tensor(sidf[:, 4, :], sidf[:, 2, :], sidf[:, 3, :], ALU.mult))
            link(V.tensor_tensor(sidf[:, 3, :], sidf[:, 0, :], sidf[:, 4, :], ALU.subtract))
            V.tensor_copy(dest[:, :], sidf[:, 3, :]).then_inc(s["dest"], 1)
            need(dve, "silu_e", 1)
            link(V.tensor_scalar(cT[:, 2, :, :], cT[:, 1, :, :], 1.0, None, ALU.add))
            link(V.reciprocal(cT[:, 1, :, :], cT[:, 2, :, :]))
            V.tensor_tensor(cT[:, 3, :, :], cT[:, 0, :, :], cT[:, 1, :, :], ALU.mult).then_inc(s["silu"], 1)
            need(dve, "wd_hi", 1)
            V.tensor_tensor(wdr[:, 1].rearrange("p k g n -> p (k g n)"), big[:, :], wdr[:, 0].bitcast(F32).rearrange("p k g n -> p (k g n)"), ALU.subtract).then_inc(s["wd_lo"], 1)
            need(dve, "modT_mm", 6)
            mt = VP[:, 0:4 * KT * B].rearrange("p (g k b) -> p g k b", g=4, k=KT)
            for n in range(4):
                link(V.tensor_scalar(modT[:, n], mt[:, n], 1.0 if n % 2 else 0.0, None, ALU.add))
            for n, bank in enumerate((QP, RP)):
                row, aux = mrow[:, n * D:(n + 1) * D], mrow2[:, n * D:(n + 1) * D]
                link(V.tensor_scalar(row, bank[0:B, :], 0.0, 2.0, ALU.is_ge, ALU.mult))
                link(V.tensor_scalar(row, row, 1.0, None, ALU.subtract))
                link(V.tensor_tensor(aux, bank[0:B, :], row, ALU.mult))
                V.scalar_tensor_tensor(out=row, in0=aux, scalar=0.25, in1=row, op0=ALU.max, op1=ALU.mult).then_inc(s["row_ev"], 1)
            with dve.Fori(0, H) as h:
                need(dve, "set_hi", h * 3 + 1)
                V.tensor_tensor(wstage[:, 3, :], rawf[:, 0, 3 * L + D:4 * L + D], wstage[:, 2, :].bitcast(F32), ALU.subtract).then_inc(s["set_lo"], 1)
                need(dve, "set_hi", h * 3 + 2)
                V.tensor_tensor(wstage[:, 1, :], QP[:, 0:P], wstage[:, 0, :].bitcast(F32), ALU.subtract).then_inc(s["set_lo"], 1)
                need(dve, "set_hi", h * 3 + 3)
                V.tensor_tensor(ow[:, 1, h, :], RP, ow[:, 0, h, :].bitcast(F32), ALU.subtract).then_inc(s["set_lo"], 1)

            def inverse_root(link, t0, n):
                v, y, a = (nr[:, k, t0:t0 + n] for k in range(3))
                bits = nr.bitcast(I32)
                link(V.tensor_scalar(v, mv[:, t0:t0 + n, 1], EPS, None, ALU.add))
                link(V.tensor_scalar(bits[:, 2, t0:t0 + n], bits[:, 0, t0:t0 + n], 1, None, ALU.logical_shift_right))
                link(V.tensor_scalar(bits[:, 1, t0:t0 + n], bits[:, 2, t0:t0 + n], -1.0, float(0x5F3759DF), ALU.mult, ALU.add))
                for step in range(STEPS):
                    link(V.scalar_tensor_tensor(out=a, in0=y, scalar=-0.5, in1=y, op0=ALU.mult, op1=ALU.mult))
                    link(V.tensor_tensor(a, a, v, ALU.mult))
                    link(V.scalar_tensor_tensor(out=y if step < STEPS - 1 else rstd[:, t0:t0 + n], in0=a, scalar=1.5, in1=y,
                                                op0=ALU.add, op1=ALU.mult))

            def rotate(head):
                need(dve, "qr_mm", head + 1)
                need(dve, "qr_lo", head)
                V.tensor_tensor(qrot, RP, cosin, ALU.mult).then_inc(s["qr_t"], 1)

            def low_query(head, parity):
                need(dve, "q_hi", head + 1)
                V.tensor_tensor(qs[:, parity, 1, :], QP, qs[:, parity, 0, :].bitcast(F32), ALU.subtract).then_inc(s["q_lo"], 1)

            def clip(head, g):
                need(dve, "s_mm", head * 3 + (g + 1))
                need(dve, "e_hi", head * 3)
                for i, c0 in GROUPS[g]:
                    n = S - i * P
                    ins = V.scalar_tensor_tensor(out=clipped[:, GOFF[g] + c0:GOFF[g] + c0 + n], in0=SC[g][:, c0:c0 + n], scalar=-CLIP,
                                                 in1=bound[:, 0:n], op0=ALU.max, op1=ALU.min)
                ins.then_inc(s["s_clip"], 1)

            def low_prob(head, parity, g):
                cols = slice(GOFF[g], GOFF[g] + GCOLS[g])
                need(dve, "e_hi", head * 3 + (g + 1))
                V.tensor_tensor(prob[:, parity, 1, cols], expo[:, cols], prob[:, parity, 0, cols].bitcast(F32), ALU.subtract).then_inc(s["e_lo"], 1)

            def normalise(head):
                need(dve, "l_mm", head + 1)
                V.reciprocal(recip[:, :], LP).then_inc(s["rec"], 1)
                need(dve, "rec", head + 1)
                need(dve, "a_lo", head)
                V.tensor_tensor(attn32[:, :], VP, recip[:, :], ALU.mult).then_inc(s["v_norm"], 1)

            def add_out(pair, t):
                need(dve, "o_mm", pair * NT + (t + 1))
                V.tensor_tensor(acc[:, t, :], acc[:, t, :], OP, ALU.add).then_inc(s["o_add"], 1)

            dve.wait_ge(s["zero_out"], 16 * (KT + 1))
            K1 = 2 * NT + NEWTON + 2
            with dve.Fori(0, B) as b:
                link = linker(dve, s["ch1"], b * K1, apart)
                V.tensor_copy(modb[:, :, :], modT[:, :, :, b]).then_inc(s["modb"], 1)
                dve.wait_ge(s["x_in"], b * 16 + 16)
                for t in range(NT):
                    link(V.bn_stats(st6[:, t, :], xb[:, t, :]))
                    link(V.bn_aggr(mv[:, t, :], st6[:, t, :]))
                inverse_root(link, 0, NT)
                for t in range(NT):
                    V.tensor_scalar(xn[:, t, :], xb[:, t, :], mv[:, t, 0:1], rstd[:, t:t + 1], ALU.subtract, ALU.mult).then_inc(s["norm"], 1)
                for k in range(KT):
                    need(dve, "h1_hi", b * KT + (k + 1))
                    V.tensor_tensor(h1r[:, 1, k, :], h1[:, k, :], h1r[:, 0, k, :].bitcast(F32), ALU.subtract).then_inc(s["h1_lo"], 1)
                need(dve, "cq_hi", b + 1)
                V.tensor_tensor(cq[:, 1, :], QP, cq[:, 0, :].bitcast(F32), ALU.subtract).then_inc(s["cq_lo"], 1)
                need(dve, "ck32", b + 1)
                V.tensor_tensor(ckT[:, 1, :], RP, ckT[:, 0, :].bitcast(F32), ALU.subtract).then_inc(s["ck_lo"], 1)
                need(dve, "kr_mm", b * 2 + 2)
                link(V.tensor_tensor(krot2, VP, coscos, ALU.mult))
                link(V.tensor_tensor(krot1, LP, sinsin, ALU.mult))
                V.tensor_tensor(krot1, krot1, krot2, ALU.add).then_inc(s["kr_t"], 1)
                need(dve, "kr_hi", b + 1)
                V.tensor_tensor(kr[:, 1, :], krot1, kr[:, 0, :].bitcast(F32), ALU.subtract).then_inc(s["kr_lo"], 1)
                need(dve, "ckt_hi", b + 1)
                V.tensor_tensor(ck[:, 1].rearrange("p t n -> p (t n)"), LP, ck[:, 0].bitcast(F32).rearrange("p t n -> p (t n)"), ALU.subtract).then_inc(s["ckt_lo"], 1)

                h = b * H
                rotate(h)
                low_query(h, 0)
                rotate(h + 1)
                low_query(h + 1, 1)
                for g in range(3):
                    clip(h, g)
                for g in range(3):
                    low_prob(h, 0, g)
                rotate(h + 2)
                low_query(h + 2, 0)
                for g in range(3):
                    clip(h + 1, g)
                for g in range(3):
                    low_prob(h + 1, 1, g)
                normalise(h)
                need(dve, "acc0", b + 1)
                apart(dve)
                with dve.Fori(1, NPAIR - 1) as p:
                    h = b * H + p * 2
                    pair = b * NPAIR + p
                    rotate(h + 1)
                    low_query(h + 1, 1)
                    for g in range(3):
                        clip(h, g)
                    for g in range(3):
                        low_prob(h, 0, g)
                    normalise(h - 1)
                    rotate(h + 2)
                    low_query(h + 2, 0)
                    for g in range(3):
                        clip(h + 1, g)
                        add_out(pair - 1, g)
                    for g in range(3):
                        low_prob(h + 1, 1, g)
                    add_out(pair - 1, 3)
                    normalise(h)
                h = b * H + (H - 2)
                pair = b * NPAIR + (NPAIR - 1)
                rotate(h + 1)
                low_query(h + 1, 1)
                for g in range(3):
                    clip(h, g)
                for g in range(3):
                    low_prob(h, 0, g)
                normalise(h - 1)
                for g in range(3):
                    clip(h + 1, g)
                    add_out(pair - 1, g)
                for g in range(3):
                    low_prob(h + 1, 1, g)
                add_out(pair - 1, 3)
                normalise(h)
                normalise(h + 1)
                dve.wait_ge(s["ga_in"], b * 16 + 16)
                for t in range(NT):
                    add_out(pair, t)
                need(dve, "o_add", (pair + 1) * NT)
                for t in range(NT):
                    V.tensor_tensor(acc[:, t, :], acc[:, t, :], grow[:, :], ALU.mult).then_inc(s["x1g"], 1)
                need(dve, "x1g", b * NT + NT)
                ins = V.tensor_tensor(acc[:, :, :], acc[:, :, :], xb[:, :, :], ALU.add).then_inc(s["x1"], 1)

            with dve.Fori(0, KT) as k:
                dve.wait_ge(s["tab_in"], k * 16 + 16)
                dve.wait_ge(s["w_in"], k * 16 + 16)
                for e in range(E):
                    if e < 2:
                        need(dve, "ew_lo", k * E)
                    V.tensor_tensor(ewf[:, e % 2, :], tab.rearrange("p (n e) -> p e n", e=E)[:, e, :], wrow, ALU.add).then_inc(s["ew_f"], 1)
                    need(dve, "ew_hi", k * E + (e + 1))
                    V.tensor_tensor(ew[:, 1, k, e, :], ewf[:, e % 2, :], ew[:, 0, k, e, :].bitcast(F32), ALU.subtract).then_inc(s["ew_lo"], 1)
            K2 = 12 + NEWTON
            with dve.Fori(0, B) as b:
                V.tensor_copy(modb[:, :, :], modT[:, :, :, b]).then_inc(s["modb2"], 1)
                dve.wait_ge(s["gb_in"], b * 16 + 16)
                apart(dve)
                with dve.Fori(0, NT // 2) as m:
                    for u in range(2):
                        t = b * NT + m * 2 + u
                        link = linker(dve, s["ch2"], t * K2, apart)
                        dve.wait_ge(s["xt_in"], (b * NT + m * 2) * 16 + 32)
                        link(V.bn_stats(st6[:, u, :], xt[u]))
                        link(V.bn_aggr(mv[:, u, :], st6[:, u, :]))
                        inverse_root(link, u, 1)
                        V.tensor_scalar(xnt[u], xt[u], mv[:, u, 0:1], rstd[:, u:u + 1], ALU.subtract, ALU.mult).then_inc(s["xnorm2"], 1)
                        need(dve, "h_hi", t + 1)
                        V.tensor_tensor(hTr[:, u, 1], hT[:, u], hTr[:, u, 0].bitcast(F32), ALU.subtract).then_inc(s["h_lo"], 1)
                        need(dve, "lg_mm", t + 1)
                        link(V.tensor_scalar(lg[:, u, :], ps[:, 7, 0:E], 50.0, -50.0, ALU.min, ALU.max))
                        link(V.max(top[:, u, :], lg[:, u, :]))
                        V.tensor_scalar(gw[:, u, 0:1], top[:, u, 1:2], top[:, u, 0:1], None, ALU.subtract).then_inc(s["lg_d"], 1)
                        link(V.max_index(topi[:, u, :], top[:, u, :], lg[:, u, :]))
                        link(V.tensor_copy(topf[:, u, :], topi[:, u, :]))
                        need(dve, "lg_e", t + 1)
                        link(V.tensor_scalar(gw[:, u, 2:3], gw[:, u, 1:2], 1.0, None, ALU.add))
                        link(V.reciprocal(gw[:, u, 3:4], gw[:, u, 2:3]))
                        link(V.tensor_tensor(gw[:, u, 4:5], gw[:, u, 1:2], gw[:, u, 3:4], ALU.mult))
                        link(V.tensor_scalar(gt[:, u, 0, :], iota8, topf[:, u, 0:1], gw[:, u, 3:4], ALU.is_equal, ALU.mult))
                        link(V.tensor_scalar(gt[:, u, 1, :], iota8, topf[:, u, 1:2], gw[:, u, 4:5], ALU.is_equal, ALU.mult))
                        V.tensor_tensor(gt[:, u, 2, :], gt[:, u, 0, :], gt[:, u, 1, :], ALU.add).then_inc(s["gates"], 1)
                        need(dve, "gates", t + 1)
                        for e in range(E):
                            need(dve, "e_mm", t * E + (e + 1))
                            if e == 0:
                                V.tensor_scalar(accE[u], ps[:, 0, :], gt[:, u, 2, 0:1], None, ALU.mult).then_inc(s["e_acc"], 1)
                            else:
                                need(dve, "e_acc", t * E + e)
                                V.scalar_tensor_tensor(out=accE[u], in0=ps[:, e % 4, :], scalar=gt[:, u, 2, e:e + 1], in1=accE[u],
                                                       op0=ALU.mult, op1=ALU.add).then_inc(s["e_acc"], 1)
                        need(dve, "e_acc", t * E + E)
                        link(V.tensor_tensor(accE[u], accE[u], grow[:, :], ALU.mult))
                        V.tensor_tensor(yt[u], accE[u], xt[u], ALU.add).then_inc(s["y"], 1)


def kernel(**inputs):
    import numpy as np
    import concourse.bacc as bacc
    from concourse.bass_utils import run_bass_kernel_spmd as run

    def g(name):
        return np.asarray(inputs[name])

    def rope_rows(a):
        return a.reshape(a.shape[:-2] + (DR // 2, 2, a.shape[-1]))[..., ::-1, :].reshape(a.shape)

    inv = np.float32(10000.0) ** (-np.arange(0, DR, 2, dtype=np.float32) / np.float32(DR))
    ang = np.arange(S, dtype=np.float32)[:, None] * inv[None, :].astype(np.float32)
    cos, sin = np.repeat(np.cos(ang).T, 2, axis=0), np.repeat(np.sin(ang).T, 2, axis=0)
    sin = sin * np.where(np.arange(DR) % 2 == 0, -1.0, 1.0)[:, None]
    consts = np.zeros((P, 5, S), np.float32)
    consts[:, 0] = np.concatenate([cos, sin])
    consts[:, 1] = np.concatenate([cos, cos])
    consts[:, 2] = np.concatenate([sin, sin])
    key, query = np.arange(P)[:, None], np.arange(S)[None, :]
    consts[:, 3] = np.where(query >= key, CLIP, -1.0e30)
    consts[:, 4, 0:P] = np.eye(P)
    consts[:, 4, P:2 * P] = 1.0
    consts[:, 4, 2 * P:3 * P] = np.arange(P)[None, :] > np.arange(P)[:, None]
    consts[:, 4, 3 * P:3 * P + 8] = np.arange(8)
    consts[:, 4, 3 * P + 8] = D * D + np.arange(P)

    wkr = g("L0_attn_W_KR")
    wkrs = rope_rows(wkr)
    wd = np.stack([g("L0_attn_W_DQ").T, g("L0_attn_W_DKV").T, np.concatenate([wkr, wkr]).T, np.concatenate([wkrs, wkrs]).T], axis=1)
    wqr = g("L0_attn_W_QR").reshape(H, DR, L)
    wqr = np.concatenate([wqr, rope_rows(wqr)], axis=1).transpose(0, 2, 1)
    idx = g("L0_ffn_mask_idx")
    arrays = {
        "x": g("L0_attn_x").reshape(B * S, D), "wd": wd, "wuq": g("L0_attn_W_UQ"), "wuk": g("L0_attn_W_UK"), "wuv": g("L0_attn_W_UV"),
        "wqr": wqr, "wo": g("L0_attn_W_O").T, "gate": g("L0_ffn_gate_w").T, "w": g("L0_ffn_W").T, "atoms": g("L0_ffn_atoms"),
        "eaw": g("L0_ffn_expert_atom_weights"),
        "imp": g("L0_ffn_importance").reshape(E, ST, P).transpose(2, 1, 0).reshape(P, ST * E),
        "idx_col": idx.reshape(ST, P).T, "idx_row": idx, "c": g("L0_c").T, "wmod": g("L0_wmod"), "consts": consts,
    }
    arrays = {f"in_{n}": np.ascontiguousarray(a) for n, a in arrays.items()}
    nc = bacc.Bacc("TRN2", target_bir_lowering=False, num_devices=1)
    args = [nc.dram_tensor(n, a.shape, mybir.dt.from_np(a.dtype), kind="ExternalInput").ap() for n, a in arrays.items()]
    args.append(nc.dram_tensor("out_0", (B * S, D), F32, kind="ExternalOutput").ap())
    build(nc, *args)
    r = run(nc, [arrays], core_ids=[0])
    return r.results[0]["out_0"].reshape(B, S, D)
```

```python
from contextlib import ExitStack

import concourse.bass as bass
from concourse import mybir

F32 = mybir.dt.float32
F32R = mybir.dt.float32r
I32 = mybir.dt.int32
U32 = mybir.dt.uint32
ALU = mybir.AluOpType
ACT = mybir.ActivationFunctionType
AX = mybir.AxisListType

B, S, D = 8, 512, 512
H, DH, DR, L = 16, 128, 64, 128
P = 128
NT = S // P
KT = D // P
E, NS, NA = 8, 4096, 64
ST = NS // P
NPAIR = H // 2
SCALE = float(DH + DR) ** -0.5
CLIP = 80.0
EPS = 1e-5
COL_BITS = D.bit_length() - 1
SCAT_B = ST // B

GROUPS = [[(0, 0)], [(1, 0), (3, S - P)], [(2, 0)]]
GCOLS = [S, S, S - 2 * P]
GOFF = [0, S, 2 * S]
PCOLS = sum(GCOLS)
PE_ORDER = [(0, 0, 0), (1, 1, 0), (1, 3, S - P), (2, 2, 0)]


CONS = 4 * P + 9
MOD_ORDER = (0, 1, 3, 4, 2, 5)
STEPS = 4
NEWTON = 3 + 3 * STEPS


def linker(eng, semaphore, base, apart=None):
    count = [0]

    def link(ins):
        count[0] += 1
        ins.then_inc(semaphore, 1)
        eng.wait_ge(semaphore, base + (count[0] + 1))
        if apart:
            apart(eng)

    return link


def build(nc, x, wd, wuq, wuk, wuv, wqr, wo, gate, w, atoms, eaw, imp, idx_col, idx_row, c, wmod, consts, out):
    ctx = ExitStack()
    with ctx:
        def sb(name, shape, dt=F32):
            return ctx.enter_context(nc.sbuf_tensor(name, shape, dt))

        def sem(name):
            return ctx.enter_context(nc.semaphore(name))

        head_w = nc.dram_tensor("head_w", [H, P, 4, P], F32, kind="Internal").ap()
        gates_d = nc.dram_tensor("gates_d", [B, 2 * D], F32, kind="Internal").ap()
        x1_d = nc.dram_tensor("x1_d", [B * S, D], F32, kind="Internal").ap()
        table_d = nc.dram_tensor("table_d", [D * D + P, E], F32, kind="Internal").ap()

        arena = sb("arena", [P, 2 * KT * E * D], F32R)
        ew = arena[:, :].rearrange("p (s k e n) -> p s k e n", s=2, k=KT, e=E)
        cut = [0]

        def take(n):
            cut[0] += n
            assert cut[0] <= 2 * KT * E * D
            return arena[:, cut[0] - n:cut[0]]

        ow = take(2 * H * D).rearrange("p (s h n) -> p s h n", s=2, h=H)
        prob = take(4 * PCOLS).rearrange("p (b s n) -> p b s n", b=2, s=2)
        qs = take(8 * S).rearrange("p (b s n) -> p b s n", b=2, s=4)
        cq = take(2 * S).rearrange("p (s n) -> p s n", s=2)
        ckT = take(2 * S).rearrange("p (s n) -> p s n", s=2)
        ck = take(2 * S).rearrange("p (s t n) -> p s t n", s=2, t=NT)
        kr = take(2 * S).rearrange("p (s n) -> p s n", s=2)
        attn = take(4 * S).rearrange("p (j s n) -> p j s n", j=2, s=2)
        wstage = prob[:, :, :, :].rearrange("p b s n -> p (b s n)")[:, 0:8 * P].rearrange("p (u s n) -> p u s n", u=2, s=4)
        hw = sb("hw", [P, 2, 4, P], F32R)
        wdr = sb("wdr", [P, 2, KT, 3, P], F32R)
        h1r = sb("h1r", [P, 2, KT, S], F32R)
        hTr = h1r[:, :, :, :].rearrange("p s k n -> p (s k n)")[:, 0:4 * KT * P].rearrange(
            "p (u s k n) -> p u s k n", u=2, s=2, k=KT)

        con = sb("con", [P, 2 * S + CONS])
        cosin, bound = con[:, 0:S], con[:, S:2 * S]
        ident, fold, later = (con[:, 2 * S + n * P:2 * S + (n + 1) * P] for n in range(3))
        iota8, trash = con[:, 2 * S + 3 * P:2 * S + 3 * P + 8], con[:, 2 * S + 3 * P + 8:2 * S + 3 * P + 9]
        ones = con[:, 2 * S + 3 * P + 9:2 * S + 4 * P + 9]
        work = sb("work", [P, 3 * NT * D])
        xres, xin, acc = (work[:, n * NT * D:(n + 1) * NT * D].rearrange("p (t n) -> p t n", t=NT) for n in range(3))
        rows = work[:, NT * D:3 * NT * D].bitcast(I32)
        rawf = work[:, 2 * NT * D:3 * NT * D].rearrange("p (u n) -> p u n", u=2)
        small = sb("small", [P, PCOLS + 3 * S])
        clipped, tmp = small[:, 0:PCOLS], small[:, PCOLS:PCOLS + 3 * S].rearrange("p (n s) -> p n s", s=S)
        expo = clipped
        mrow, mrow2 = small[0:B, 0:2 * D], small[0:B, 2 * D:4 * D]
        ck32, krot = small[:, 0:S], small[:, S:2 * S]
        qrot, h1t = tmp[:, 0, :], [tmp[:, 0, :], tmp[:, 1, :]]
        wmb = [a.rearrange("p (k n) -> p k n", k=KT) for a in (work[:, 0:NT * D], small[:, 0:NT * D])]
        esum = tmp[:, 2, :]
        eq = tmp[:, 2, :].rearrange("p (u a n) -> p u a n", u=2, a=2)
        wdraw = work[:, 0:KT * 3 * P].rearrange("p (k g n) -> p k g n", k=KT, g=3)
        wrows = small[:, 0:KT * D].rearrange("p (k n) -> p k n", k=KT)
        hT = small[:, 0:2 * KT * P].rearrange("p (u k n) -> p u k n", u=2, k=KT)
        zeros = sb("zeros", [P, P])[:, :]
        grow = sb("grow", [P, D])
        cT = grow[:, 0:4 * KT * B].rearrange("p (a k b) -> p a k b", a=4, k=KT)
        went = grow[:, 4 * KT * B:4 * KT * B + ST * E].rearrange("p (t e) -> p t e", e=E)
        sidx = grow[:, D - 4 * ST:D].bitcast(I32).rearrange("p (a t) -> p a t", a=4)
        st6 = sb("st6", [P, NT, 6])
        mv = sb("mv", [P, NT, 2])
        rstd = sb("rstd", [P, NT])
        rl = sb("rl", [P, 2, NT])
        nr = sb("nr", [P, 3, NT])
        modT = sb("modT", [P, 4, KT, B])
        modb = sb("modb", [P, 4, KT])
        gate_sb = sb("gate_sb", [P, KT, E])
        went2 = sb("went2", [P, ST, E])
        wcur = sb("wcur", [P, 1, E])
        smx = sb("smx", [E, 3, NA])
        sms = sb("sms", [E, 4])
        smT = sb("smT", [NA, E])
        sidf = sb("sidf", [P, 5, ST])
        dest = sb("dest", [P, ST], U32)
        dcur = sb("dcur", [P, 1], U32)
        top = sb("top", [P, 2, 8])
        topi = sb("topi", [P, 2, 8], U32)
        topf = sb("topf", [P, 2, 8])
        gw = sb("gw", [P, 2, 5])
        gt = sb("gt", [P, 2, 3, E])
        lg = sb("lg", [P, 2, E])
        atoms_sb = [work[0:NA, 0:NS // 2], small[0:NA, 3 * ST * E:3 * ST * E + NS // 2]]
        sig = clipped[:, 0:3 * ST * E].rearrange("p (a t e) -> p a t e", a=3, e=E)

        ps = ctx.enter_context(nc.psum_tensor("ps", [P, 8, S], F32))
        setA, setB = [ps[:, 3, 0:P], ps[:, 0, 0:P]], [ps[:, 4, :], ps[:, 1, :]]
        SC = [ps[:, 0, :], ps[:, 1, :], ps[:, 2, :]]
        QP, RP, VP = ps[:, 3, :], ps[:, 4, :], ps[:, 5, :]
        OP = [ps[:, 6, :], ps[:, 7, :]]
        LC = ps[:, 2, 2 * P:2 * P + NT]

        names = """con_in c_in wd_in wd_hi wd_lo g_in silu_e silu modT_mm modT_ev row_mm row_ev gates_out
             setA setB set_hi set_lo
            eaw_in at_mm imp_in imp_e sm_e sm sm_tr smT_ev ent idx_in rows_in eq eq_mm dest zero_set zero_out scat cur later
            x_in xr_in ga_in modb bn bn_aggr root newton norm tr h1_ev h1_hi h1_lo cq_mm ck_mm kr_mm cq_hi cq_lo ck_hi ck32 ck_lo ckt_mm ckt_hi ckt_lo kr_t kr_fold kr_hi kr_lo
            q_mm qr_mm q_hi q_lo qr_t qr_hi qr_lo s_mm s_clip e32 e_hi e_lo pv_mm esum esum_step lcol rl a_hi a_lo o_mm o_add x1g x1_dve x1 x1_out
            ch0 ch1 ch2 w_in ew_f ew_f_pool ew_hi ew_lo gb_in modb2 xnorm2 tr2 h_ev h_hi h_lo lg_mm lg_d lg_e gates
            passed gated e_mm e_acc y""".split()
        s = {n: sem(n) for n in names}
        counters = [n for n in names if not n.endswith(("_in", "_out")) and n not in ("scat", "passed")]

        free = {"e_acc": 4, "o_add": 1, "x1": NT, "ew_lo": 4, "set_hi": 3, "set_lo": 3}

        def need(eng, name, n):
            eng.wait_ge(s[name], n + 1)

        def apart(eng):
            eng.sem_inc(s["passed"], 1)

        w_slot = [sem(f"head_w_in{n}") for n in range(2)]
        atoms_in = [sem(f"atoms_in{n}") for n in range(2)]
        mod_slot = [sem(f"mod_in{n}") for n in range(2)]
        raw_slot = [sem(f"raw_in{n}") for n in range(2)]
        set_slot = [sem(f"set_out{n}") for n in range(2)]
        tab_slot = [sem(f"tab_in{n}") for n in range(4)]
        x_slot = [sem(f"xt_in{n}") for n in range(NT)]
        y_slot = [sem(f"y_out{n}") for n in range(NT)]
        block = ctx.enter_context(nc.Block())

        x_t = x.rearrange("(b t p) d -> b p t d", t=NT, p=P)
        x1_t = x1_d.rearrange("(b t p) d -> b p t d", t=NT, p=P)
        x1_tile = x1_d.rearrange("(n p) d -> n p d", p=P)
        out_tile = out.rearrange("(n p) d -> n p d", p=P)
        wmod_t = wmod.rearrange("(k p) (g n) -> g p k n", p=P, g=6)
        wuq_t, wuk_t, wuv_t = (a.rearrange("(h d) l -> h d l", d=DH) for a in (wuq, wuk, wuv))
        wo_t = wo.rearrange("(h d) n -> h d n", d=DH)
        table_quarter = table_d[0:D * D, :].rearrange("(k p f r) e -> k f p r e", k=KT, p=P, f=4)

        xt = [xres[:, n, :] for n in range(NT)]
        yt = [xin[:, n, :] for n in range(NT)]
        xnt, accE = [acc[:, n, :] for n in range(2)], [acc[:, 2 + n, :] for n in range(2)]
        QD = D // 4
        tab = [work[:, (n + 2) * QD * E:(n + 3) * QD * E].rearrange("p (n e) -> p n e", e=E) for n in range(4)]

        def dense_piece(k, n):
            return wrows[:, k, n * QD:(n + 1) * QD].rearrange("p (n e) -> p n e", e=1).broadcast_to([P, QD, E])

        w_rows = w.rearrange("(k p) n -> p k n", p=P)

        @block.sync
        def _(sp):
            sp.dma_start(smx[:, 0, :], eaw).then_inc(s["eaw_in"], 16)
            for name in counters:
                sp.sem_inc(s[name], 1 + free.get(name, 0))
            for stored in y_slot + set_slot:
                sp.sem_inc(stored, 1)
            sp.dma_start(sig[:, 0, :, :].rearrange("p t e -> p (t e)"), imp).then_inc(s["imp_in"], 16)
            sp.dma_start(cT[:, 0, :, :], c.rearrange("(k p) b -> p k b", p=P)).then_inc(s["c_in"], 16)
            sp.dma_start(con[:, :], consts).then_inc(s["con_in"], 16)
            for half in range(2):
                sp.dma_start(atoms_sb[half], atoms[:, half * (NS // 2):(half + 1) * (NS // 2)]).then_inc(atoms_in[half], 16)
            sp.dma_start(sidx[:, 0, :], idx_col).then_inc(s["idx_in"], 16)
            sp.dma_start(rows, idx_row.partition_broadcast(P)).then_inc(s["rows_in"], 16)
            sp.dma_start(gate_sb[:, :, :], gate.rearrange("(k p) e -> p k e", p=P)).then_inc(s["g_in"], 16)
            need(sp, "at_mm", 1)
            for g in range(6):
                if g == 1:
                    need(sp, "ent", 1)
                if g > 1:
                    need(sp, "modT_mm", g - 1)
                sp.dma_start(wmb[g % 2], wmod_t[MOD_ORDER[g]]).then_inc(mod_slot[g % 2], 16)
            need(sp, "modT_mm", 5)
            sp.dma_start(wdraw, wd.rearrange("(k p) g n -> p k g n", p=P)).then_inc(s["wd_in"], 16)

            def head_raw(h, u):
                for n, src in enumerate((wuq_t, wuk_t, wuv_t)):
                    sp.dma_start(rawf[:, u, n * L:(n + 1) * L], src[h]).then_inc(raw_slot[u], 16)
                sp.dma_start(rawf[:, u, 3 * L:3 * L + D], wo_t[h]).then_inc(raw_slot[u], 16)
                sp.dma_start(rawf[:, u, 3 * L + D:4 * L + D], wqr[h]).then_inc(raw_slot[u], 16)

            def store_head(h, u):
                need(sp, "set_hi", h * 3 + 6)
                need(sp, "set_lo", h * 3 + 6)
                sp.dma_start(head_w[h], wstage[:, u].bitcast(F32)).then_inc(set_slot[u], 16)

            need(sp, "dest", 1)
            for u in range(2):
                head_raw(u, u)
            sp.dma_start(xin, x_t[0]).then_inc(s["x_in"], 16)
            need(sp, "row_ev", 2)
            sp.dma_start(gates_d, mrow).then_inc(s["gates_out"], 16)
            with sp.Fori(0, H // 2 - 1) as m:
                for u in range(2):
                    store_head(m * 2 + u, u)
                    head_raw(m * 2 + (u + 2), u)
            for u in range(2):
                sp.wait_ge(set_slot[u], 16 * (H // 2 - 1) + 1)
                sp.dma_start(hw[:, u].bitcast(F32), head_w[u]).then_inc(w_slot[u], 16)
            for u in range(2):
                store_head(H - 2 + u, u)
            for u in range(2):
                sp.wait_ge(set_slot[u], 16 * (H // 2) + 1)
            sp.wait_ge(s["gates_out"], 16)
            need(sp, "wd_lo", 1)

            def next_weights(used, head, slot):
                need(sp, "qr_mm", used)
                sp.dma_start(hw[:, slot].bitcast(F32), head_w[head]).then_inc(w_slot[slot], 16)

            def load_tokens(b):
                sp.dma_start(xin, x_t[b]).then_inc(s["x_in"], 16)

            def load_residual(b):
                sp.dma_start(xres, x_t[b]).then_inc(s["xr_in"], 16)
                sp.dma_start(grow[:, :], gates_d[b, 0:D].partition_broadcast(P)).then_inc(s["ga_in"], 16)

            def store_x1(b):
                need(sp, "x1", b * NT + 2 * NT)
                sp.dma_start(x1_t[b], xres).then_inc(s["x1_out"], 16)
                sp.wait_ge(s["x1_out"], b * 16 + 16)

            def weights_of_batch(b):
                with sp.Fori(0, (H - 6) // 2) as m:
                    for j in range(2):
                        next_weights(b * H + m * 2 + (4 + j), m * 2 + (5 + j), 1 - j)
                for j in range(3):
                    next_weights(b * H + (H - 2 + j), (H - 1 + j) % H, 1 - j % 2)

            need(sp, "tr", KT)
            load_tokens(1)
            need(sp, "zero_set", 1)
            for k in range(KT):
                if k < 3:
                    next_weights(1 + k, 2 + k, k % 2)
                sp.dma_start(table_d[k * D * P:(k + 1) * D * P, :].rearrange("(p r a) e -> p r (a e)", p=P, a=P // E),
                             zeros.rearrange("p (r n) -> p r n", r=1).broadcast_to([P, D * E // P, P])).then_inc(s["zero_out"], 16)
            sp.dma_start(table_d[D * D:D * D + P, :], zeros[:, 0:E]).then_inc(s["zero_out"], 16)
            load_residual(0)

            def batch(b, more):
                weights_of_batch(b)
                need(sp, "tr", b * KT + 2 * KT)
                if more:
                    load_tokens(b + 2)
                for j in range(3):
                    next_weights(b * H + (H + 1 + j), 2 + j, j % 2)
                store_x1(b)
                if more:
                    apart(sp)
                load_residual(b + 1)

            with sp.Fori(0, B - 2) as b:
                batch(b, True)
            batch(B - 2, False)
            weights_of_batch(B - 1)
            def table_piece(k, n):
                sp.dma_start(tab[n], table_quarter[k, n]).then_inc(tab_slot[n], 16)

            sp.wait_ge(s["scat"], 16 * ST)
            need(sp, "tr", B * KT)
            for n in range(2):
                table_piece(0, n)
            need(sp, "o_add", B * (H * NT) + 1)
            sp.dma_start(wrows, w_rows).then_inc(s["w_in"], 16)
            need(sp, "x1", B * NT + NT)
            for n in range(2, 4):
                table_piece(0, n)
            store_x1(B - 1)
            for slot in range(2):
                sp.wait_ge(w_slot[slot], 16 * (B * NPAIR + 1))
            for n in range(NT):
                sp.dma_start(xt[n], x1_tile[n]).then_inc(x_slot[n], 16)
            with sp.Fori(1, KT) as k:
                for n in range(4):
                    need(sp, "ew_lo", k * 4 + (n + 1))
                    table_piece(k, n)
            need(sp, "ew_lo", KT * 4 + 4)

            def outputs(b, t, n, more):
                need(sp, "y", t + 1)
                sp.dma_start(out_tile[t], yt[n]).then_inc(y_slot[n], 16)
                if more:
                    sp.dma_start(xt[n], x1_tile[t + NT]).then_inc(x_slot[n], 16)

            with sp.Fori(0, B - 1) as b:
                need(sp, "y", b * NT)
                sp.dma_start(grow[:, :], gates_d[b, D:2 * D].partition_broadcast(P)).then_inc(s["gb_in"], 16)
                for n in range(NT):
                    outputs(b, b * NT + n, n, True)
            sp.dma_start(grow[:, :], gates_d[B - 1, D:2 * D].partition_broadcast(P)).then_inc(s["gb_in"], 16)
            for n in range(NT):
                outputs(B - 1, (B - 1) * NT + n, n, False)
            for n in range(NT):
                sp.wait_ge(y_slot[n], 16 * B + 1)

        @block.gpsimd
        def _(pool):
            pool.memset(zeros, 0.0).then_inc(s["zero_set"], 1)
            need(pool, "dest", 1)

            def low_rope(head, parity):
                need(pool, "qr_hi", head + 1)
                pool.tensor_tensor(qs[:, parity, 3, :], qrot, qs[:, parity, 2, :].bitcast(F32), ALU.subtract).then_inc(s["qr_lo"], 1)

            def scatter(n):
                pool.wait_ge(s["zero_out"], 16 * (KT + 1))
                pool.tensor_copy(dcur[:, :], dest[:, bass.ds(n, 1)]).then_inc(s["cur"], 1)
                pool.tensor_copy(wcur[:, 0, :], went2[:, bass.ds(n, 1), :]).then_inc(s["cur"], 1)
                need(pool, "cur", n * 2 + 2)
                apart(pool)
                pool.indirect_dma_start(table_d, bass.IndirectOffsetOnAxis(ap=dcur[:, 0:1], axis=0), wcur[:, 0, :], None,
                                        compute_op=ALU.add).then_inc(s["scat"], 16)

            def scattered(n):
                pool.wait_ge(s["scat"], n * 16 + 16)
                apart(pool)

            def residual(b, some):
                if some[0] == 0:
                    pool.wait_ge(s["ga_in"], b * 16 + 16)
                    pool.wait_ge(s["xr_in"], b * 16 + 16)
                for t in some:
                    need(pool, "o_add", b * (H * NT) + (H - 1) * NT + (t + 2))
                    pool.tensor_tensor(acc[:, t, :], acc[:, t, :], grow[:, :], ALU.mult).then_inc(s["x1g"], 1)
                    need(pool, "x1g", b * NT + (t + 1))
                    pool.tensor_tensor(xres[:, t, :], xres[:, t, :], acc[:, t, :], ALU.add).then_inc(s["x1"], 1)

            def newton(b):
                v, y, a = (nr[:, k, :] for k in range(3))
                need(pool, "root", b + 1)
                link = linker(pool, s["newton"], b * (4 * STEPS), apart)
                for n in range(STEPS):
                    link(pool.tensor_tensor(a, y, y, ALU.mult))
                    link(pool.tensor_tensor(a, a, v, ALU.mult))
                    link(pool.tensor_scalar(a, a, -0.5, 1.5, ALU.mult, ALU.add))
                    link(pool.tensor_tensor(y if n < STEPS - 1 else rstd[:, :], a, y, ALU.mult))

            def sum_first(h):
                need(pool, "lcol", h)
                need(pool, "e32", h * 3 + 1)
                apart(pool)
                pool.tensor_copy(esum[:, 0:P], expo[:, 0:P]).then_inc(s["esum_step"], 1)

            def sum_rest(h):
                need(pool, "e32", h * 3 + 2)
                pool.tensor_tensor(esum[:, P:S], expo[:, P:S], expo[:, S:2 * S - P], ALU.add).then_inc(s["esum_step"], 1)
                need(pool, "esum_step", h * 3 + 2)
                pool.tensor_tensor(esum[:, 3 * P:S], esum[:, 3 * P:S], expo[:, 2 * S - P:2 * S], ALU.add).then_inc(s["esum_step"], 1)
                need(pool, "esum_step", h * 3 + 3)
                need(pool, "e32", h * 3 + 3)
                pool.tensor_tensor(esum[:, 2 * P:S], esum[:, 2 * P:S], expo[:, 2 * S:PCOLS], ALU.add).then_inc(s["esum"], 1)

            def step(h, parity, q=True):
                if q:
                    low_rope(h + 1, 1 - parity)
                sum_first(h)
                sum_rest(h)

            def heads(b, tokens):
                with pool.Fori(0, SCAT_B - 1) as m:
                    for n in range(2):
                        step(b * H + m * 4 + (n + 2), n)
                    scatter(b * SCAT_B + m)
                    for n in range(2):
                        step(b * H + m * 4 + (n + 4), n)
                    scattered(b * SCAT_B + m)
                if tokens is not None:
                    newton(tokens)
                step(b * H + (H - 2), 0)
                scatter(b * SCAT_B + (SCAT_B - 1))
                step(b * H + (H - 1), 1, q=False)
                scattered(b * SCAT_B + (SCAT_B - 1))

            def first_heads(h, b):
                for n in range(2):
                    low_rope(h + (n + 1), 1 - n)
                    sum_first(h + n)
                    sum_rest(h + n)
                    if b is not None:
                        residual(b, (n * 2, n * 2 + 1))

            newton(0)
            low_rope(0, 0)
            first_heads(0, None)
            with pool.Fori(0, B - 1) as b:
                heads(b, b + 1)
                low_rope(b * H + H, 0)
                first_heads(b * H + H, b)
            heads(B - 1, None)
            residual(B - 1, range(NT // 2))

            pool.wait_ge(s["w_in"], 16)
            with pool.Fori(0, KT) as k:
                for n in (0, 2):
                    pool.wait_ge(tab_slot[n], k * 16 + 16)
                    pool.tensor_tensor(tab[n], tab[n], dense_piece(k, n), ALU.add).then_inc(s["ew_f_pool"], 1)


        @block.scalar
        def _(act):
            def copy(dst, src, done):
                act.activation(dst, src, ACT.Copy).then_inc(s[done], 1)

            need(act, "sm", 1)
            act.activation(smx[:, 1, :], smx[:, 0, :], ACT.Exp, bias=sms[:, 0:1], accum_out=sms[:, 1:2]).then_inc(s["sm_e"], 1)
            act.wait_ge(s["imp_in"], 16)
            act.activation(sig[:, 1, :, :], sig[:, 0, :, :], ACT.Exp, scale=-1.0).then_inc(s["imp_e"], 1)
            act.wait_ge(s["c_in"], 16)
            act.activation(cT[:, 1, :, :], cT[:, 0, :, :], ACT.Exp, scale=-1.0).then_inc(s["silu_e"], 1)
            act.wait_ge(s["wd_in"], 16)
            copy(wdr[:, 0], wdraw, "wd_hi")
            with act.Fori(0, H // 2) as m:
                for u in range(2):
                    act.wait_ge(raw_slot[u], m * 80 + 80)
                    act.wait_ge(set_slot[u], m * 16 + 1)
                    copy(wstage[:, u, 2, :], rawf[:, u, 3 * L + D:4 * L + D], "set_hi")
                    need(act, "setA", m * 2 + (u + 1))
                    copy(wstage[:, u, 0, :], setA[u], "set_hi")
                    need(act, "setB", m * 2 + (u + 1))
                    act.activation(ow[:, 0, m * 2 + u, :], setB[u], ACT.Copy).then_inc(s["set_hi"], 1)

            def high_query(head, parity):
                need(act, "q_mm", head + 1)
                copy(qs[:, parity, 0, :], QP, "q_hi")
                need(act, "qr_t", head + 1)
                copy(qs[:, parity, 2, :], qrot, "qr_hi")

            def exps(head, parity, g):
                cols = slice(GOFF[g], GOFF[g] + GCOLS[g])
                need(act, "s_clip", head * 3 + (g + 1))
                act.activation(prob[:, parity, 0, cols], clipped[:, cols], ACT.Exp, scale=SCALE).then_inc(s["e_hi"], 1)
                need(act, "e_hi", head * 3 + (g + 1))
                act.activation(expo[:, cols], clipped[:, cols], ACT.Exp, scale=SCALE).then_inc(s["e32"], 1)

            def high_attn(head, j):
                need(act, "pv_mm", head + 1)
                copy(attn[:, j, 0, :], VP, "a_hi")

            def high_token(b, k):
                need(act, "tr", b * KT + (k + 1))
                need(act, "modb", b + 1)
                if k == 0:
                    need(act, "qr_lo", b * H)
                if k >= 2:
                    need(act, "h1_lo", b * KT + (k - 1))
                act.activation(h1t[k % 2], [QP, RP][k % 2], ACT.Identity,
                               bias=modb[:, 0, k:k + 1], scale=modb[:, 1, k:k + 1]).then_inc(s["h1_ev"], 1)
                need(act, "h1_ev", b * KT + (k + 1))
                copy(h1r[:, 0, k, :], h1t[k % 2], "h1_hi")

            def latents(b, h):
                need(act, "cq_mm", b + 1)
                copy(cq[:, 0, :], QP, "cq_hi")
                need(act, "ck_mm", b + 1)
                copy(ckT[:, 0, :], RP, "ck_hi")
                if h is not None:
                    need(act, "e_lo", h * 3)
                copy(ck32, RP, "ck32")
                if h is not None:
                    high_attn(h - 1, 1)
                high_query(b * H, 0)
                need(act, "kr_fold", b + 1)
                copy(kr[:, 0, :], SC[1], "kr_hi")
                need(act, "ckt_mm", b + 1)
                act.activation(ck[:, 0, :, :], SC[2].rearrange("p (t n) -> p t n", t=NT), ACT.Copy).then_inc(s["ckt_hi"], 1)

            def step(h, parity, q=True, v=True, e=True, tokens=None):
                if q:
                    high_query(h + 1, 1 - parity)
                for g in range(3):
                    if e:
                        exps(h, parity, g)
                    if tokens is not None:
                        high_token(tokens, g)
                if tokens is not None:
                    high_token(tokens, 3)
                if v:
                    high_attn(h - 1, 1 - parity)

            def heads(b, tokens):
                step(b * H + 1, 1)
                with act.Fori(1, NPAIR - 1) as p:
                    h = b * H + p * 2
                    step(h, 0)
                    step(h + 1, 1)
                step(b * H + (H - 2), 0)
                step(b * H + (H - 1), 1, q=False, tokens=tokens)

            for k in range(KT):
                high_token(0, k)
            act.wait_ge(s["gates_out"], 16)
            for u in range(2):
                act.wait_ge(set_slot[u], 16 * (H // 2) + 1)
            latents(0, None)
            step(0, 0, v=False)
            with act.Fori(0, B - 1) as b:
                heads(b, b + 1)
                latents(b + 1, b * H + H)
                step(b * H + H, 0, v=False)
            heads(B - 1, None)
            high_attn(B * H - 1, 1)

            with act.Fori(0, KT) as k:
                for n in range(4):
                    need(act, "ew_f" if n % 2 else "ew_f_pool", k * 2 + (n // 2 + 1))
                    act.activation(ew[:, 0, k, :, n * QD:(n + 1) * QD], tab[n].rearrange("p n e -> p e n"),
                                   ACT.Copy).then_inc(s["ew_hi"], 1)

            def modulate(t, u):
                need(act, "tr2", t + 1)
                for k in range(KT):
                    act.activation(hT[:, u, k, :], ps[:, 6, k * P:(k + 1) * P], ACT.Identity,
                                   bias=modb[:, 2, k:k + 1], scale=modb[:, 3, k:k + 1]).then_inc(s["h_ev"], 1)
                need(act, "h_ev", t * KT + KT)
                act.activation(hTr[:, u, 0, :, :], hT[:, u, :, :], ACT.Copy).then_inc(s["h_hi"], 1)
                need(act, "lg_d", t + 1)
                act.activation(gw[:, u, 1:2], gw[:, u, 0:1], ACT.Exp).then_inc(s["lg_e"], 1)

            need(act, "modb2", 1)
            modulate(0, 0)
            with act.Fori(0, B - 1) as b:
                for n in range(1, NT):
                    modulate(b * NT + n, n % 2)
                need(act, "modb2", b + 2)
                modulate(b * NT + NT, 0)
            for n in range(1, NT):
                modulate((B - 1) * NT + n, n % 2)

        @block.tensor
        def _(pe):
            def split3(o, wgt, act_, first=True, last=True):
                pe.matmul(o, wgt(0), act_(0), start=first, stop=False)
                pe.matmul(o, wgt(1), act_(0), start=False, stop=False)
                return pe.matmul(o, wgt(0), act_(1), start=False, stop=last)

            pe.wait_ge(s["con_in"], 16)
            need(pe, "sm", 2)
            pe.transpose(VP[0:NA, 0:E], smx[:, 2, :], ident[0:E, 0:E]).then_inc(s["sm_tr"], 1)
            need(pe, "smT_ev", 1)
            for half in range(2):
                pe.wait_ge(atoms_in[half], 16)
                for n in range(ST // 2):
                    t = half * (ST // 2) + n
                    mm = pe.matmul(SC[0][:, t * E:(t + 1) * E], atoms_sb[half][:, n * P:(n + 1) * P], smT[:, :], start=True, stop=True)
                mm.then_inc(s["at_mm"], 1)
            need(pe, "ent", 1)
            need(pe, "silu", 1)
            for m in range(ST // 2):
                for u in range(2):
                    need(pe, "eq", m * 2 + (u + 1))
                    pe.matmul(SC[1 + u][:, m * E:(m + 1) * E], eq[:, u, 0, :], went[:, m * 2 + u, :], start=True, stop=True).then_inc(s["eq_mm"], 1)
                g, n = m // KT, m % KT
                if n == 0:
                    pe.wait_ge(mod_slot[g % 2], 16 * (g // 2 + 1))
                for k in range(KT):
                    mm = pe.matmul(VP[:, (g * KT + n) * B:(g * KT + n + 1) * B], wmb[g % 2][:, k, n * P:(n + 1) * P], cT[:, 3, k, :],
                                   start=(k == 0), stop=(k == KT - 1))
                if n == KT - 1:
                    mm.then_inc(s["modT_mm"], 1)
            for g in range(2):
                pe.wait_ge(mod_slot[g], 48)
                for k in range(KT):
                    mm = pe.matmul((QP, RP)[g][0:B, :], cT[:, 3, k, :], wmb[g][:, k, :], start=(k == 0), stop=(k == KT - 1))
                mm.then_inc(s["modT_mm"], 1)
            need(pe, "row_ev", 2)
            with pe.Fori(0, H // 2) as m:
                for u in range(2):
                    pe.wait_ge(raw_slot[u], m * 80 + 80)
                    need(pe, "set_hi", m * 6 + u * 3)
                    need(pe, "set_lo", m * 6 + u * 3)
                    pe.matmul(setA[u], rawf[:, u, 0:L], rawf[:, u, L:2 * L], start=True, stop=True).then_inc(s["setA"], 1)
                    pe.matmul(setB[u], rawf[:, u, 2 * L:3 * L], rawf[:, u, 3 * L:3 * L + D], start=True, stop=True).then_inc(s["setB"], 1)
            need(pe, "set_hi", 3 * H + 3)
            need(pe, "set_lo", 3 * H + 3)
            need(pe, "wd_lo", 1)

            def queries(head, parity, nw):
                pe.wait_ge(w_slot[parity], nw * 16 + 16)
                need(pe, "q_hi", head)
                need(pe, "q_lo", head)
                split3(QP, lambda i: hw[:, parity, i, :], lambda i: cq[:, i, :]).then_inc(s["q_mm"], 1)
                need(pe, "qr_t", head)
                split3(RP, lambda i: hw[:, parity, 2 + i, :], lambda i: cq[:, i, :]).then_inc(s["qr_mm"], 1)

            def scores(head, parity, g):
                if g == 0:
                    need(pe, "q_lo", head + 1)
                    need(pe, "qr_lo", head + 1)
                need(pe, "s_clip", head * 3)
                if g == 2:
                    need(pe, "rl", head)
                for i, c0 in GROUPS[g]:
                    n = S - i * P
                    o = SC[g][:, c0:c0 + n]
                    keys = slice(i * P, (i + 1) * P)
                    split3(o, lambda k: ckT[:, k, keys], lambda k: qs[:, parity, k, i * P:S], last=False)
                    mm = split3(o, lambda k: kr[:, k, keys], lambda k: qs[:, parity, 2 + k, i * P:S], first=False)
                mm.then_inc(s["s_mm"], 1)

            def values(head, parity):
                need(pe, "a_lo", head)
                for n, (g, i, c0) in enumerate(PE_ORDER):
                    if n != 2:
                        need(pe, "e_lo", head * 3 + (g + 1))
                    cols = slice(GOFF[g] + c0, GOFF[g] + c0 + S - i * P)
                    mm = split3(VP[:, i * P:S], lambda k: ck[:, k, i, :], lambda k: prob[:, parity, k, cols], first=(n == 0), last=(n == 3))
                mm.then_inc(s["pv_mm"], 1)

            def columns_of_sums(head):
                need(pe, "esum", head + 1)
                need(pe, "rl", head)
                need(pe, "s_clip", head * 3 + 3)
                for t in range(NT):
                    mm = pe.matmul(LC[:, t:t + 1], esum[:, t * P:(t + 1) * P], ones[:, 0:1], start=True, stop=True)
                mm.then_inc(s["lcol"], 1)

            def project(head, j, place, t):
                if t == 0:
                    need(pe, "a_lo", head + 1)
                need(pe, "o_add", head * NT + t)
                split3(OP[t % 2], lambda k: attn[:, j, k, t * P:(t + 1) * P], lambda k: ow[:, k, place, :]).then_inc(s["o_mm"], 1)

            def transpose_tokens(b, k):
                need(pe, "norm", b * NT + NT)
                if k >= 2:
                    need(pe, "h1_ev", b * KT + (k - 1))
                for t in range(NT):
                    mm = pe.transpose([QP, RP][k % 2][:, t * P:(t + 1) * P], xin[:, t, k * P:(k + 1) * P], ident)
                mm.then_inc(s["tr"], 1)

            def down(b, bank, g, done):
                for k in range(KT):
                    if g == 0:
                        need(pe, "h1_lo", b * KT + (k + 1))
                    mm = split3(bank, lambda i: wdr[:, i, k, g, :], lambda i: h1r[:, i, k, :], first=(k == 0), last=(k == KT - 1))
                mm.then_inc(s[done], 1)

            def latents(b, h):
                def out(t):
                    if h is not None:
                        project(h - 2, 0, H - 2, t)

                if h is not None:
                    columns_of_sums(h - 1)
                need(pe, "h1_ev", b * KT + 3)
                down(b, QP, 0, "cq_mm")
                out(0)
                down(b, RP, 1, "ck_mm")
                out(1)
                if h is not None:
                    values(h - 1, 1)
                out(2)
                if h is not None:
                    need(pe, "s_clip", h * 3)
                down(b, SC[0], 2, "kr_mm")
                out(3)
                need(pe, "cq_lo", b + 1)
                need(pe, "ck_lo", b + 1)
                queries(b * H, 0, b * NPAIR)
                need(pe, "kr_t", b + 1)
                pe.matmul(SC[1], fold, krot, start=True, stop=True).then_inc(s["kr_fold"], 1)
                need(pe, "ck32", b + 1)
                if h is not None:
                    need(pe, "rl", h)
                for t in range(NT):
                    mm = pe.transpose(SC[2][:, t * P:(t + 1) * P], ck32[:, t * P:(t + 1) * P], ident)
                mm.then_inc(s["ckt_mm"], 1)

            def step(h, parity, nw=None, v=None, o=None, sc=True, tokens=None, first=None):
                if nw is not None:
                    queries(h + 1, 1 - parity, nw)
                if first is not None:
                    need(pe, "kr_lo", first + 1)
                    need(pe, "ckt_lo", first + 1)
                if v:
                    columns_of_sums(v[0])
                for g in range(3):
                    if sc:
                        scores(h, parity, g)
                    if tokens is not None:
                        transpose_tokens(tokens, g)
                    if o:
                        project(*o, g)
                if tokens is not None:
                    transpose_tokens(tokens, 3)
                if v:
                    values(*v)
                if o:
                    project(*o, 3)

            def heads(b, tokens):
                h = b * H
                step(h + 1, 1, nw=b * NPAIR + 1, v=(h, 0))
                with pe.Fori(1, NPAIR - 1) as p:
                    h = b * H + p * 2
                    pair = b * NPAIR + p
                    step(h, 0, nw=pair, v=(h - 1, 1), o=(h - 2, 0, p * 2 - 2))
                    step(h + 1, 1, nw=pair + 1, v=(h, 0), o=(h - 1, 1, p * 2 - 1))
                h = b * H + (H - 2)
                step(h, 0, nw=b * NPAIR + (NPAIR - 1), v=(h - 1, 1), o=(h - 2, 0, H - 4))
                step(h + 1, 1, v=(h, 0), o=(h - 1, 1, H - 3), tokens=tokens)

            for k in range(KT):
                transpose_tokens(0, k)
            latents(0, None)
            step(0, 0, nw=0, first=0)
            with pe.Fori(0, B - 1) as b:
                heads(b, b + 1)
                h = b * H + H
                latents(b + 1, h)
                step(h, 0, nw=b * NPAIR + NPAIR, first=b + 1, o=(h - 1, 1, H - 1))
            heads(B - 1, None)
            h = B * H
            step(None, 0, v=(h - 1, 1), o=(h - 2, 0, H - 2), sc=False)
            step(None, 1, o=(h - 1, 1, H - 1), sc=False)

            need(pe, "ew_lo", KT * 4 + 4)
            need(pe, "ew_hi", KT * 4)
            pe.wait_ge(s["g_in"], 16)

            def transposes(t, u):
                need(pe, "xnorm2", t + 1)
                need(pe, "h_ev", t * KT)
                for k in range(KT):
                    mm = pe.transpose(ps[:, 6, k * P:(k + 1) * P], xnt[u][:, k * P:(k + 1) * P], ident)
                mm.then_inc(s["tr2"], 1)

            def logits(t, u):
                need(pe, "h_lo", t + 1)
                need(pe, "gates", t)
                for k in range(KT):
                    mm = pe.matmul(ps[:, 7, 0:E], hT[:, u, k, :], gate_sb[:, k, :], start=(k == 0), stop=(k == KT - 1))
                mm.then_inc(s["lg_mm"], 1)

            def experts(t, u, some):
                for e in some:
                    need(pe, "e_acc", t * E + (e + 1))
                    for k in range(KT):
                        mm = split3(ps[:, e % 4, :], lambda i: hTr[:, u, i, k, :], lambda i: ew[:, i, k, e, :],
                                    first=(k == 0), last=(k == KT - 1))
                    mm.then_inc(s["e_mm"], 1)

            def token_tile(t, u, more):
                experts(t, u, range(0, 4))
                if more:
                    transposes(t + 1, 1 - u)
                experts(t, u, range(4, 6))
                if more:
                    logits(t + 1, 1 - u)
                experts(t, u, range(6, E))

            transposes(0, 0)
            logits(0, 0)
            with pe.Fori(0, B - 1) as b:
                for n in range(NT):
                    token_tile(b * NT + n, n % 2, True)
            for n in range(NT):
                token_tile((B - 1) * NT + n, n % 2, n < NT - 1)

        @block.vector
        def _(dve):
            V = nc.vector
            link = linker(dve, s["ch0"], 0)
            dve.wait_ge(s["eaw_in"], 16)
            link(V.tensor_reduce(sms[:, 2:3], smx[:, 0, :], AX.X, ALU.max))
            V.tensor_scalar(sms[:, 0:1], sms[:, 2:3], -1.0, None, ALU.mult).then_inc(s["sm"], 1)
            need(dve, "sm_e", 1)
            link(V.reciprocal(sms[:, 3:4], sms[:, 1:2]))
            V.tensor_scalar(smx[:, 2, :], smx[:, 1, :], sms[:, 3:4], None, ALU.mult).then_inc(s["sm"], 1)
            need(dve, "sm_tr", 1)
            V.tensor_copy(smT[:, :], VP[0:NA, 0:E]).then_inc(s["smT_ev"], 1)
            need(dve, "imp_e", 1)
            link(V.tensor_scalar(sig[:, 2, :, :], sig[:, 1, :, :], 1.0, None, ALU.add))
            link(V.reciprocal(sig[:, 1, :, :], sig[:, 2, :, :]))
            need(dve, "at_mm", 2)
            V.tensor_tensor(went[:, :, :].rearrange("p t e -> p (t e)"), SC[0][:, 0:ST * E], sig[:, 1, :, :].rearrange("p t e -> p (t e)"), ALU.mult).then_inc(s["ent"], 1)
            need(dve, "silu_e", 1)
            link(V.tensor_scalar(cT[:, 2, :, :], cT[:, 1, :, :], 1.0, None, ALU.add))
            link(V.reciprocal(cT[:, 1, :, :], cT[:, 2, :, :]))
            V.tensor_tensor(cT[:, 3, :, :], cT[:, 0, :, :], cT[:, 1, :, :], ALU.mult).then_inc(s["silu"], 1)
            dve.wait_ge(s["con_in"], 16)
            dve.wait_ge(s["idx_in"], 16)
            link(V.tensor_scalar(sidx[:, 1, :], sidx[:, 0, :], D - 1, COL_BITS, ALU.bitwise_and, ALU.logical_shift_left))
            link(V.tensor_scalar(sidx[:, 2, :], sidx[:, 0, :], COL_BITS, None, ALU.logical_shift_right))
            link(V.tensor_tensor(sidx[:, 3, :], sidx[:, 1, :], sidx[:, 2, :], ALU.bitwise_or))
            link(V.tensor_copy(sidf[:, 0, :], sidx[:, 3, :]))
            link(V.tensor_copy(sidf[:, 1, :], sidx[:, 0, :]))
            dve.wait_ge(s["rows_in"], 16)
            with dve.Fori(0, ST // 2) as m:
                need(dve, "eq_mm", m * 2)
                need(dve, "later", m * 2)
                for u in range(2):
                    here = rows[:, bass.ds((m * 2 + u) * P, P)]
                    col = sidf[:, 1, bass.ds(m * 2 + u, 1)]
                    V.tensor_scalar(eq[:, u, 0, :], here, col, None, ALU.is_equal).then_inc(s["eq"], 1)
                    V.scalar_tensor_tensor(out=eq[:, u, 1, :], in0=here, scalar=col, in1=later, op0=ALU.is_equal, op1=ALU.mult,
                                           accum_out=sidf[:, 2, bass.ds(m * 2 + u, 1)]).then_inc(s["later"], 1)
            need(dve, "later", ST)
            need(dve, "eq_mm", ST)
            w2 = went2[:, :, :].rearrange("p (m u) e -> p u m e", u=2)
            for u in range(2):
                link(V.tensor_copy(w2[:, u], SC[1 + u][:, 0:ST // 2 * E].rearrange("p (m e) -> p m e", e=E)))
            link(V.tensor_scalar(sidf[:, 3, :], sidf[:, 2, :], 0.0, None, ALU.is_gt))
            link(V.tensor_scalar(sidf[:, 2, :], sidf[:, 0, :], trash, None, ALU.subtract))
            link(V.tensor_tensor(sidf[:, 4, :], sidf[:, 2, :], sidf[:, 3, :], ALU.mult))
            link(V.tensor_tensor(sidf[:, 3, :], sidf[:, 0, :], sidf[:, 4, :], ALU.subtract))
            V.tensor_copy(dest[:, :], sidf[:, 3, :]).then_inc(s["dest"], 1)
            need(dve, "modT_mm", 6)
            mt = VP[:, 0:4 * KT * B].rearrange("p (g k b) -> p g k b", g=4, k=KT)
            for n in range(4):
                link(V.tensor_scalar(modT[:, n], mt[:, n], 1.0 if n % 2 else 0.0, None, ALU.add))
            for n, bank in enumerate((QP, RP)):
                row, aux = mrow[:, n * D:(n + 1) * D], mrow2[:, n * D:(n + 1) * D]
                link(V.tensor_scalar(row, bank[0:B, :], 0.0, 2.0, ALU.is_ge, ALU.mult))
                link(V.tensor_scalar(row, row, 1.0, None, ALU.subtract))
                link(V.tensor_tensor(aux, bank[0:B, :], row, ALU.mult))
                V.scalar_tensor_tensor(out=row, in0=aux, scalar=0.25, in1=row, op0=ALU.max, op1=ALU.mult).then_inc(s["row_ev"], 1)
            def inverse_root(link, t0, n):
                v, y, a = (nr[:, k, t0:t0 + n] for k in range(3))
                first_root(link, t0, n, None)
                for step in range(STEPS):
                    link(V.scalar_tensor_tensor(out=a, in0=y, scalar=-0.5, in1=y, op0=ALU.mult, op1=ALU.mult))
                    link(V.tensor_tensor(a, a, v, ALU.mult))
                    link(V.scalar_tensor_tensor(out=y if step < STEPS - 1 else rstd[:, t0:t0 + n], in0=a, scalar=1.5, in1=y,
                                                op0=ALU.add, op1=ALU.mult))

            def first_root(link, t0, n, done):
                v = nr[:, 0, t0:t0 + n]
                bits = nr.bitcast(I32)
                link(V.tensor_scalar(v, mv[:, t0:t0 + n, 1], EPS, None, ALU.add))
                link(V.tensor_scalar(bits[:, 2, t0:t0 + n], bits[:, 0, t0:t0 + n], 1, None, ALU.logical_shift_right))
                ins = V.tensor_scalar(bits[:, 1, t0:t0 + n], bits[:, 2, t0:t0 + n], -1.0, float(0x5F3759DF), ALU.mult, ALU.add)
                if done:
                    ins.then_inc(s[done], 1)
                else:
                    link(ins)

            def rotate(head):
                need(dve, "qr_mm", head + 1)
                need(dve, "qr_lo", head)
                V.tensor_tensor(qrot, RP, cosin, ALU.mult).then_inc(s["qr_t"], 1)

            def low_query(head, parity):
                need(dve, "q_hi", head + 1)
                V.tensor_tensor(qs[:, parity, 1, :], QP, qs[:, parity, 0, :].bitcast(F32), ALU.subtract).then_inc(s["q_lo"], 1)

            def clip(head, g):
                need(dve, "s_mm", head * 3 + (g + 1))
                need(dve, "e_lo", head * 3)
                need(dve, "esum", head)
                for i, c0 in GROUPS[g]:
                    n = S - i * P
                    ins = V.scalar_tensor_tensor(out=clipped[:, GOFF[g] + c0:GOFF[g] + c0 + n], in0=SC[g][:, c0:c0 + n], scalar=-CLIP,
                                                 in1=bound[:, 0:n], op0=ALU.max, op1=ALU.min)
                ins.then_inc(s["s_clip"], 1)

            def low_prob(head, parity, g):
                cols = slice(GOFF[g], GOFF[g] + GCOLS[g])
                need(dve, "e32", head * 3 + (g + 1))
                V.tensor_tensor(prob[:, parity, 1, cols], expo[:, cols], prob[:, parity, 0, cols].bitcast(F32), ALU.subtract).then_inc(s["e_lo"], 1)

            def low_attn(head, j):
                need(dve, "a_hi", head + 1)
                V.tensor_tensor(attn[:, j, 1, :], VP, attn[:, j, 0, :].bitcast(F32), ALU.subtract).then_inc(s["a_lo"], 1)

            def inverse_sums(head, parity):
                need(dve, "lcol", head + 1)
                V.reciprocal(rl[:, parity, :], LC).then_inc(s["rl"], 1)

            def add_out(head, parity, t, first=None):
                need(dve, "o_mm", head * NT + (t + 1))
                if t == 0:
                    need(dve, "rl", head + 1)
                if first is not None:
                    need(dve, "x1", first * NT + (t + 1))
                    V.tensor_scalar(acc[:, t, :], OP[t % 2], rl[:, parity, t:t + 1], None, ALU.mult).then_inc(s["o_add"], 1)
                    return
                V.scalar_tensor_tensor(out=acc[:, t, :], in0=OP[t % 2], scalar=rl[:, parity, t:t + 1], in1=acc[:, t, :],
                                       op0=ALU.mult, op1=ALU.add).then_inc(s["o_add"], 1)

            def statistics_of(b):
                V.tensor_copy(modb[:, :, :], modT[:, :, :, b]).then_inc(s["modb"], 1)
                dve.wait_ge(s["x_in"], b * 16 + 16)
                for t in range(NT):
                    V.bn_stats(st6[:, t, :], xin[:, t, :]).then_inc(s["bn"], 1)

            def deviation_of(b):
                link = linker(dve, s["ch1"], b * K1, apart)
                need(dve, "bn", b * NT + NT)
                apart(dve)
                for t in range(NT):
                    V.bn_aggr(mv[:, t, :], st6[:, t, :]).then_inc(s["bn_aggr"], 1)
                need(dve, "bn_aggr", b * NT + NT)
                first_root(link, 0, NT, "root")

            def normalise(b):
                need(dve, "newton", (b + 1) * (4 * STEPS))
                for t in range(NT):
                    V.tensor_scalar(xin[:, t, :], xin[:, t, :], mv[:, t, 0:1], rstd[:, t:t + 1], ALU.subtract, ALU.mult).then_inc(s["norm"], 1)

            def low_token(b, k):
                need(dve, "h1_hi", b * KT + (k + 1))
                V.tensor_tensor(h1r[:, 1, k, :], h1t[k % 2], h1r[:, 0, k, :].bitcast(F32), ALU.subtract).then_inc(s["h1_lo"], 1)

            def latents(b, h):
                def out(t):
                    if h is not None:
                        add_out(h - 2, 0, t)

                if h is not None:
                    need(dve, "o_add", (h - 2) * NT + 1)
                    inverse_sums(h - 1, 1)
                need(dve, "cq_hi", b + 1)
                V.tensor_tensor(cq[:, 1, :], QP, cq[:, 0, :].bitcast(F32), ALU.subtract).then_inc(s["cq_lo"], 1)
                out(0)
                need(dve, "ck32", b + 1)
                V.tensor_tensor(ckT[:, 1, :], RP, ckT[:, 0, :].bitcast(F32), ALU.subtract).then_inc(s["ck_lo"], 1)
                out(1)
                if h is not None:
                    low_attn(h - 1, 1)
                out(2)
                need(dve, "kr_mm", b + 1)
                V.tensor_tensor(krot, SC[0], cosin, ALU.mult).then_inc(s["kr_t"], 1)
                out(3)
                rotate(b * H)
                low_query(b * H, 0)
                need(dve, "kr_hi", b + 1)
                V.tensor_tensor(kr[:, 1, :], SC[1], kr[:, 0, :].bitcast(F32), ALU.subtract).then_inc(s["kr_lo"], 1)
                need(dve, "ckt_hi", b + 1)
                V.tensor_tensor(ck[:, 1].rearrange("p t n -> p (t n)"), SC[2], ck[:, 0].bitcast(F32).rearrange("p t n -> p (t n)"), ALU.subtract).then_inc(s["ckt_lo"], 1)

            def step(h, parity, q=True, sc=True, v=None, o=None, tokens=None, norm=None, first=None, ready=None):
                if q:
                    rotate(h + 1)
                    low_query(h + 1, 1 - parity)
                if ready is not None:
                    deviation_of(ready)
                if v and o:
                    need(dve, "o_add", o[0] * NT + 1)
                if v:
                    inverse_sums(*v)
                for g in range(3):
                    if sc:
                        clip(h, g)
                    if o:
                        add_out(*o, g, first)
                    if tokens is not None and g:
                        low_token(tokens, g - 1)
                if sc:
                    low_prob(h, parity, 0)
                    low_prob(h, parity, 1)
                if tokens is not None:
                    low_token(tokens, 2)
                if o:
                    add_out(*o, 3, first)
                if tokens is not None:
                    low_token(tokens, 3)
                if sc:
                    low_prob(h, parity, 2)
                if norm is not None:
                    normalise(norm)
                if v:
                    low_attn(*v)

            def heads(b, tokens):
                h = b * H
                step(h + 1, 1, v=(h, 0))
                if tokens is not None:
                    statistics_of(tokens)
                step(h + 2, 0, v=(h + 1, 1), o=(h, 0), first=b, ready=tokens)
                step(h + 3, 1, v=(h + 2, 0), o=(h + 1, 1))
                with dve.Fori(2, NPAIR - 1) as p:
                    h = b * H + p * 2
                    step(h, 0, v=(h - 1, 1), o=(h - 2, 0))
                    step(h + 1, 1, v=(h, 0), o=(h - 1, 1))
                h = b * H + (H - 2)
                step(h, 0, v=(h - 1, 1), o=(h - 2, 0), norm=tokens)
                step(h + 1, 1, q=False, v=(h, 0), o=(h - 1, 1), tokens=tokens)

            K1 = 2
            statistics_of(0)
            deviation_of(0)
            need(dve, "wd_hi", 1)
            V.tensor_tensor(wdr[:, 1].rearrange("p k g n -> p (k g n)"), wdraw.rearrange("p k g n -> p (k g n)"), wdr[:, 0].bitcast(F32).rearrange("p k g n -> p (k g n)"), ALU.subtract).then_inc(s["wd_lo"], 1)
            with dve.Fori(0, H // 2) as m:
                for u in range(2):
                    h = m * 2 + u
                    need(dve, "set_hi", h * 3 + 4)
                    V.tensor_tensor(wstage[:, u, 3, :], rawf[:, u, 3 * L + D:4 * L + D], wstage[:, u, 2, :].bitcast(F32), ALU.subtract).then_inc(s["set_lo"], 1)
                    need(dve, "set_hi", h * 3 + 5)
                    V.tensor_tensor(wstage[:, u, 1, :], setA[u], wstage[:, u, 0, :].bitcast(F32), ALU.subtract).then_inc(s["set_lo"], 1)
                    need(dve, "set_hi", h * 3 + 6)
                    V.tensor_tensor(ow[:, 1, h, :], setB[u], ow[:, 0, h, :].bitcast(F32), ALU.subtract).then_inc(s["set_lo"], 1)

            normalise(0)
            for k in range(KT):
                low_token(0, k)
            latents(0, None)
            step(0, 0)
            with dve.Fori(0, B - 1) as b:
                heads(b, b + 1)
                h = b * H + H
                latents(b + 1, h)
                step(h, 0, o=(h - 1, 1))
            heads(B - 1, None)
            h = B * H
            step(None, 0, q=False, sc=False, v=(h - 1, 1), o=(h - 2, 0))
            step(None, 1, q=False, sc=False, o=(h - 1, 1))

            dve.wait_ge(s["ga_in"], B * 16)
            dve.wait_ge(s["xr_in"], B * 16)
            need(dve, "o_add", B * (H * NT) + 1)
            for t in range(NT // 2, NT):
                V.tensor_tensor(acc[:, t, :], acc[:, t, :], grow[:, :], ALU.mult).then_inc(s["x1_dve"], 1)
            for n, t in enumerate(range(NT // 2, NT)):
                need(dve, "x1_dve", n + 1)
                V.tensor_tensor(xres[:, t, :], xres[:, t, :], acc[:, t, :], ALU.add).then_inc(s["x1"], 1)

            K2 = 11 + NEWTON

            def chain(t, start):
                link = linker(dve, s["ch2"], t * K2 + start, apart)
                return link

            def statistics(b, t, n):
                u = n % 2
                link = chain(t, 0)
                dve.wait_ge(x_slot[n], b * 16 + 16)
                link(V.bn_stats(st6[:, u, :], xt[n]))
                link(V.bn_aggr(mv[:, u, :], st6[:, u, :]))
                inverse_root(link, u, 1)

            def scale_tokens(t, n):
                u = n % 2
                V.tensor_scalar(xnt[u], xt[n], mv[:, u, 0:1], rstd[:, u:u + 1], ALU.subtract, ALU.mult).then_inc(s["xnorm2"], 1)

            dve.wait_ge(s["w_in"], 16)

            def table_tile(k):
                def add_dense(n):
                    dve.wait_ge(tab_slot[n], k * 16 + 16)
                    V.tensor_tensor(tab[n], tab[n], dense_piece(k, n), ALU.add).then_inc(s["ew_f"], 1)

                def low_weights(n):
                    need(dve, "ew_hi", k * 4 + (n + 1))
                    high, low = (ew[:, i, k, :, n * QD:(n + 1) * QD] for i in range(2))
                    V.tensor_tensor(low, tab[n].rearrange("p n e -> p e n"), high.bitcast(F32), ALU.subtract).then_inc(s["ew_lo"], 1)

                add_dense(1)
                low_weights(0)
                low_weights(1)
                add_dense(3)
                low_weights(2)
                low_weights(3)

            with dve.Fori(0, KT // 2) as k:
                table_tile(k)
            V.tensor_copy(modb[:, :, :], modT[:, :, :, 0]).then_inc(s["modb2"], 1)
            statistics(0, 0, 0)
            with dve.Fori(KT // 2, KT) as k:
                table_tile(k)
            def low_tokens(t, u):
                need(dve, "h_hi", t + 1)
                V.tensor_tensor(hTr[:, u, 1], hT[:, u], hTr[:, u, 0].bitcast(F32), ALU.subtract).then_inc(s["h_lo"], 1)

            def top_two(t, u):
                link = chain(t, 2 + NEWTON)
                need(dve, "lg_mm", t + 1)
                link(V.tensor_scalar(lg[:, u, :], ps[:, 7, 0:E], 50.0, -50.0, ALU.min, ALU.max))
                link(V.max(top[:, u, :], lg[:, u, :]))
                V.tensor_scalar(gw[:, u, 0:1], top[:, u, 1:2], top[:, u, 0:1], None, ALU.subtract).then_inc(s["lg_d"], 1)
                link(V.max_index(topi[:, u, :], top[:, u, :], lg[:, u, :]))
                link(V.tensor_copy(topf[:, u, :], topi[:, u, :]))

            def gates_of(t, u):
                link = chain(t, 6 + NEWTON)
                need(dve, "lg_e", t + 1)
                link(V.tensor_scalar(gw[:, u, 2:3], gw[:, u, 1:2], 1.0, None, ALU.add))
                link(V.reciprocal(gw[:, u, 3:4], gw[:, u, 2:3]))
                link(V.tensor_tensor(gw[:, u, 4:5], gw[:, u, 1:2], gw[:, u, 3:4], ALU.mult))
                link(V.tensor_scalar(gt[:, u, 0, :], iota8, topf[:, u, 0:1], gw[:, u, 3:4], ALU.is_equal, ALU.mult))
                link(V.tensor_scalar(gt[:, u, 1, :], iota8, topf[:, u, 1:2], gw[:, u, 4:5], ALU.is_equal, ALU.mult))
                V.tensor_tensor(gt[:, u, 2, :], gt[:, u, 0, :], gt[:, u, 1, :], ALU.add).then_inc(s["gates"], 1)

            def add_experts(t, u, some):
                for e in some:
                    need(dve, "e_mm", t * E + (e + 1))
                    if e == 0:
                        need(dve, "gates", t + 1)
                        V.tensor_scalar(accE[u], ps[:, 0, :], gt[:, u, 2, 0:1], None, ALU.mult).then_inc(s["e_acc"], 1)
                    else:
                        need(dve, "e_acc", t * E + (e + 4))
                        V.scalar_tensor_tensor(out=accE[u], in0=ps[:, e % 4, :], scalar=gt[:, u, 2, e:e + 1], in1=accE[u],
                                               op0=ALU.mult, op1=ALU.add).then_inc(s["e_acc"], 1)

            def token_tile(b, n, b_next, more):
                t, u = b * NT + n, n % 2
                n_next = (n + 1) % NT
                if more:
                    if n_next == 0:
                        V.tensor_copy(modb[:, :, :], modT[:, :, :, b_next]).then_inc(s["modb2"], 1)
                    statistics(b_next, t + 1, n_next)
                    scale_tokens(t + 1, n_next)
                add_experts(t, u, range(0, 5))
                if more:
                    low_tokens(t + 1, 1 - u)
                add_experts(t, u, range(5, 6))
                if more:
                    top_two(t + 1, 1 - u)
                add_experts(t, u, range(6, 7))
                if more:
                    gates_of(t + 1, 1 - u)
                add_experts(t, u, range(7, E))
                need(dve, "e_acc", t * E + (E + 4))
                if n == 0:
                    dve.wait_ge(s["gb_in"], b * 16 + 16)
                    if not isinstance(b, int):
                        apart(dve)
                linker(dve, s["gated"], t, apart)(V.tensor_tensor(accE[u], accE[u], grow[:, :], ALU.mult))
                dve.wait_ge(y_slot[n], b * 16 + 1)
                V.tensor_tensor(yt[n], accE[u], xt[n], ALU.add).then_inc(s["y"], 1)

            need(dve, "ew_lo", KT * 4 + 4)
            scale_tokens(0, 0)
            low_tokens(0, 0)
            top_two(0, 0)
            gates_of(0, 0)
            with dve.Fori(0, B - 1) as b:
                for n in range(NT):
                    token_tile(b, n, b if n < NT - 1 else b + 1, True)
            for n in range(NT):
                token_tile(B - 1, n, B - 1, n < NT - 1)


def kernel(**inputs):
    import numpy as np
    import concourse.bacc as bacc
    from concourse.bass_utils import run_bass_kernel_spmd as run

    def g(name):
        return np.asarray(inputs[name])

    def rope_rows(a):
        return a.reshape(a.shape[:-2] + (DR // 2, 2, a.shape[-1]))[..., ::-1, :].reshape(a.shape)

    inv = np.float32(10000.0) ** (-np.arange(0, DR, 2, dtype=np.float32) / np.float32(DR))
    ang = np.arange(S, dtype=np.float32)[:, None] * inv[None, :].astype(np.float32)
    cos, sin = np.repeat(np.cos(ang).T, 2, axis=0), np.repeat(np.sin(ang).T, 2, axis=0)
    sin = sin * np.where(np.arange(DR) % 2 == 0, -1.0, 1.0)[:, None]
    consts = np.zeros((P, 2 * S + CONS), np.float32)
    key, query, col = np.arange(P)[:, None], np.arange(S)[None, :], np.arange(P)[None, :]
    consts[:, 0:S] = np.concatenate([cos, sin])
    consts[:, S:2 * S] = np.where(query >= key, CLIP, -1.0e30)
    tail = consts[:, 2 * S:]
    tail[:, 0:P] = np.eye(P)
    tail[:, P:2 * P] = key % DR == col % DR
    tail[:, 2 * P:3 * P] = col > key
    tail[:, 3 * P:3 * P + 8] = np.arange(8)
    tail[:, 3 * P + 8] = D * D + np.arange(P)
    tail[:, 3 * P + 9:] = 1.0

    wkr = g("L0_attn_W_KR")
    wd = np.stack([g("L0_attn_W_DQ").T, g("L0_attn_W_DKV").T, np.concatenate([wkr, rope_rows(wkr)]).T], axis=1)
    wqr = g("L0_attn_W_QR").reshape(H, DR, L)
    wqr = np.concatenate([wqr, rope_rows(wqr)], axis=1).transpose(0, 2, 1)
    idx = g("L0_ffn_mask_idx")
    arrays = {
        "x": g("L0_attn_x").reshape(B * S, D), "wd": wd, "wuq": g("L0_attn_W_UQ"), "wuk": g("L0_attn_W_UK"), "wuv": g("L0_attn_W_UV"),
        "wqr": wqr, "wo": g("L0_attn_W_O").T, "gate": g("L0_ffn_gate_w").T, "w": g("L0_ffn_W").T, "atoms": g("L0_ffn_atoms"),
        "eaw": g("L0_ffn_expert_atom_weights"),
        "imp": g("L0_ffn_importance").reshape(E, ST, P).transpose(2, 1, 0).reshape(P, ST * E),
        "idx_col": idx.reshape(ST, P).T, "idx_row": idx, "c": g("L0_c").T, "wmod": g("L0_wmod"), "consts": consts,
    }
    arrays = {f"in_{n}": np.ascontiguousarray(a) for n, a in arrays.items()}
    nc = bacc.Bacc("TRN2", target_bir_lowering=False, num_devices=1)
    args = [nc.dram_tensor(n, a.shape, mybir.dt.from_np(a.dtype), kind="ExternalInput").ap() for n, a in arrays.items()]
    args.append(nc.dram_tensor("out_0", (B * S, D), F32, kind="ExternalOutput").ap())
    build(nc, *args)
    r = run(nc, [arrays], core_ids=[0])
    return r.results[0]["out_0"].reshape(B, S, D)
```
